# Optimizing a Trainium2 kernel written in Bass

```python
import numpy as np
import jax
import jax.numpy as jnp

def _softmax(x, axis=-1):
    return jax.nn.softmax(x, axis=axis)

def _gelu(x):
    return jax.nn.gelu(x, approximate=True)

def _silu(x):
    return jax.nn.silu(x)

def _sigmoid(x):
    return jax.nn.sigmoid(x)

def _layernorm(x, axis=-1, eps=1e-05):
    m = jnp.mean(x, axis=axis, keepdims=True)
    v = jnp.var(x, axis=axis, keepdims=True)
    return (x - m) / jnp.sqrt(v + eps)

def _scatter_add(tgt, idx, src, axis=0):
    return tgt.at[idx].add(src)

def _segment_sum(src, seg, n):
    return jax.ops.segment_sum(src, seg, n)
kernel_name = 'mk_decoder_preln_d1_seqx_r2_4d025f'

def setup_inputs(seed: int=0):
    np.random.seed(seed)
    _w = jnp.asarray

    def _rec_inputs():
        import jax
        import jax.numpy as jnp
        _rk = jax.random.key(seed)
        x = 0.0002417 + 0.9998 * jax.random.normal(jax.random.fold_in(_rk, 1), (32, 224, 512), jnp.float32)
        _lenS = 224 - jax.random.randint(jax.random.fold_in(_rk, 7), (32,), 0, max(1, 224 // 4) + 1, jnp.int32)
        _lenS2 = 750 - jax.random.randint(jax.random.fold_in(_rk, 8), (32,), 0, max(1, 750 // 4) + 1, jnp.int32)
        _ctx_1024P = jax.random.normal(jax.random.fold_in(_rk, 11), (32, 16, 512), jnp.float32)
        _ctx_1024c = jax.random.dirichlet(jax.random.fold_in(_rk, 511), 0.3 * jnp.ones((16,), jnp.float32), (32, 750))
        _ctx_1024t = jnp.einsum('bsk,bkd->bsd', _ctx_1024c, _ctx_1024P)
        _ctx_1024t = _ctx_1024t * jax.lax.rsqrt(jnp.mean(jnp.square(_ctx_1024t)) + 1e-12) * 0.953939
        ctx_1024 = 7.22013e-05 + 1.00017 * (_ctx_1024t + 0.3 * jax.random.normal(jax.random.fold_in(_rk, 611), (32, 750, 512), jnp.float32))
        return (x, ctx_1024)
    x, ctx_1024 = _rec_inputs()

    def _L0_attn_setup():
        import jax, jax.numpy as jnp
        import numpy as np
        NUM_HEADS = 16
        key = jax.random.key(seed)
        ks = jax.random.split(key, 6)
        B, S, D = (2, 1024, 512)
        x = jax.random.normal(ks[0], (B, S, D), dtype=jnp.float32)
        s = 1.0 / np.sqrt(D)
        Wq = jax.random.normal(ks[1], (D, D), dtype=jnp.float32) * s
        Wk = jax.random.normal(ks[2], (D, D), dtype=jnp.float32) * s
        Wv = jax.random.normal(ks[3], (D, D), dtype=jnp.float32) * s
        Wff = jax.random.normal(ks[4], (D, D), dtype=jnp.float32) * s
        bff = jax.random.normal(ks[5], (D,), dtype=jnp.float32) * 0.01
        return {'x': x, 'Wq': Wq, 'Wk': Wk, 'Wv': Wv, 'Wff': Wff, 'bff': bff}
    _L0_attn_all = _L0_attn_setup()
    _L0_attn_in = {k: v for k, v in _L0_attn_all.items() if k in ('Wq', 'Wk', 'Wv', 'Wff', 'bff')}
    del _L0_attn_all

    def _L0_xattn_setup():
        import jax, jax.numpy as jnp
        import numpy as np
        D_MODEL = 512
        B, S = (4, 1024)
        key = jax.random.key(seed)
        ks = jax.random.split(key, 10)
        s = 1.0 / np.sqrt(D_MODEL)
        return {'k': jax.random.normal(ks[0], (B, S, D_MODEL), jnp.float32), 'v': jax.random.normal(ks[1], (B, S, D_MODEL), jnp.float32), 'q': jax.random.normal(ks[2], (B, S, D_MODEL), jnp.float32), 'Wk': jax.random.normal(ks[3], (D_MODEL, D_MODEL), jnp.float32) * s, 'Wv': jax.random.normal(ks[4], (D_MODEL, D_MODEL), jnp.float32) * s, 'bv': jnp.zeros((D_MODEL,), jnp.float32), 'Wq': jax.random.normal(ks[5], (D_MODEL, D_MODEL), jnp.float32) * s, 'bq': jnp.zeros((D_MODEL,), jnp.float32), 'Wo': jax.random.normal(ks[6], (D_MODEL, D_MODEL), jnp.float32) * s, 'bo': jnp.zeros((D_MODEL,), jnp.float32)}
    _L0_xattn_all = _L0_xattn_setup()
    _L0_xattn_in = {k: v for k, v in _L0_xattn_all.items() if k in ('Wk', 'Wv', 'bv', 'Wq', 'bq', 'Wo', 'bo')}
    del _L0_xattn_all

    def _L0_ffn_setup():
        import math
        import jax, jax.numpy as jnp
        import numpy as np
        B, S, H, BOT, RD, N, K = (4, 1024, 512, 128, 48, 2048, 8)
        key = jax.random.key(seed)
        ks = jax.random.split(key, 12)
        hidden_states = jax.random.normal(ks[0], (B, S, H), jnp.float32)
        q_proj_w = jax.random.normal(ks[1], (BOT, H), jnp.float32) * (1.0 / math.sqrt(H))
        router_w = jax.random.normal(ks[2], (RD, BOT), jnp.float32) * (1.0 / math.sqrt(BOT))
        aux_keys = jax.random.normal(ks[3], (N, BOT), jnp.float32) * 0.01
        aux_values = jax.random.normal(ks[4], (N, H), jnp.float32) * 0.02
        reliability_mask = jax.random.uniform(ks[5], (N,), jnp.float32)
        unc_w1 = jax.random.normal(ks[6], (H // 4, H), jnp.float32) * (1.0 / math.sqrt(H))
        unc_b1 = jnp.zeros((H // 4,), jnp.float32)
        unc_w2 = jax.random.normal(ks[7], (1, H // 4), jnp.float32) * 0.02
        unc_b2 = jnp.zeros((1,), jnp.float32)
        gate_w1 = jnp.asarray(0.5, jnp.float32)
        gate_bias = jnp.asarray(-1.0, jnp.float32)
        return {'hidden_states': hidden_states, 'q_proj_w': q_proj_w, 'router_w': router_w, 'aux_keys': aux_keys, 'aux_values': aux_values, 'reliability_mask': reliability_mask, 'unc_w1': unc_w1, 'unc_b1': unc_b1, 'unc_w2': unc_w2, 'unc_b2': unc_b2, 'gate_w1': gate_w1, 'gate_bias': gate_bias}
    _L0_ffn_all = _L0_ffn_setup()
    _L0_ffn_in = {k: v for k, v in _L0_ffn_all.items() if k in ('q_proj_w', 'router_w', 'aux_keys', 'aux_values', 'reliability_mask', 'unc_w1', 'unc_b1', 'unc_w2', 'unc_b2', 'gate_w1', 'gate_bias')}
    del _L0_ffn_all
    return {'x': x, 'ctx_1024': ctx_1024, 'L0_attn_Wq': _L0_attn_in['Wq'], 'L0_attn_Wk': _L0_attn_in['Wk'], 'L0_attn_Wv': _L0_attn_in['Wv'], 'L0_attn_Wff': _L0_attn_in['Wff'], 'L0_attn_bff': _L0_attn_in['bff'], 'L0_xattn_Wk': _L0_xattn_in['Wk'], 'L0_xattn_Wv': _L0_xattn_in['Wv'], 'L0_xattn_bv': _L0_xattn_in['bv'], 'L0_xattn_Wq': _L0_xattn_in['Wq'], 'L0_xattn_bq': _L0_xattn_in['bq'], 'L0_xattn_Wo': _L0_xattn_in['Wo'], 'L0_xattn_bo': _L0_xattn_in['bo'], 'L0_ffn_q_proj_w': _L0_ffn_in['q_proj_w'], 'L0_ffn_router_w': _L0_ffn_in['router_w'], 'L0_ffn_aux_keys': _L0_ffn_in['aux_keys'], 'L0_ffn_aux_values': _L0_ffn_in['aux_values'], 'L0_ffn_reliability_mask': _L0_ffn_in['reliability_mask'], 'L0_ffn_unc_w1': _L0_ffn_in['unc_w1'], 'L0_ffn_unc_b1': _L0_ffn_in['unc_b1'], 'L0_ffn_unc_w2': _L0_ffn_in['unc_w2'], 'L0_ffn_unc_b2': _L0_ffn_in['unc_b2'], 'L0_ffn_gate_w1': _L0_ffn_in['gate_w1'], 'L0_ffn_gate_bias': _L0_ffn_in['gate_bias']}

def reference(x, ctx_1024, L0_attn_Wq, L0_attn_Wk, L0_attn_Wv, L0_attn_Wff, L0_attn_bff, L0_xattn_Wk, L0_xattn_Wv, L0_xattn_bv, L0_xattn_Wq, L0_xattn_bq, L0_xattn_Wo, L0_xattn_bo, L0_ffn_q_proj_w, L0_ffn_router_w, L0_ffn_aux_keys, L0_ffn_aux_values, L0_ffn_reliability_mask, L0_ffn_unc_w1, L0_ffn_unc_b1, L0_ffn_unc_w2, L0_ffn_unc_b2, L0_ffn_gate_w1, L0_ffn_gate_bias):
    import jax
    import jax.numpy as jnp

    def _L0_attn_ref(x, Wq, Wk, Wv, Wff, bff):
        import jax, jax.numpy as jnp
        import numpy as np
        NUM_HEADS = 16
        B, S, D = x.shape
        H = NUM_HEADS
        Dh = D // H
        q = x @ Wq.T * (1.0 / jnp.sqrt(jnp.asarray(D, x.dtype)))
        k = x @ Wk.T
        v = x @ Wv.T
        q = q.reshape(B, S, H, Dh)
        k = k.reshape(B, S, H, Dh)
        v = v.reshape(B, S, H, Dh)
        scores = jnp.einsum('bqhd,bkhd->bhqk', q, k)
        attn = jax.nn.softmax(scores, axis=-1)
        out = jnp.einsum('bhqk,bkhd->bqhd', attn, v).reshape(B, S, D)
        return out @ Wff.T + bff

    def _L0_xattn_ref(k, v, q, Wk, Wv, bv, Wq, bq, Wo, bo):
        import jax, jax.numpy as jnp
        import numpy as np
        D_MODEL = 512
        B, S = (4, 1024)
        kp = jnp.einsum('bsd,ed->bse', k, Wk)
        vp = jnp.einsum('bsd,ed->bse', v, Wv) + bv
        qp = jnp.einsum('bsd,ed->bse', q, Wq) + bq
        scale = 1.0 / jnp.sqrt(jnp.float32(kp.shape[-1]))
        scores = jnp.einsum('bqd,bkd->bqk', qp, kp) * scale
        probs = jax.nn.softmax(scores, axis=-1)
        ctx = jnp.einsum('bqk,bkd->bqd', probs, vp)
        return jnp.einsum('bqd,ed->bqe', ctx, Wo) + bo

    def _L0_ffn_ref(hidden_states, q_proj_w, router_w, aux_keys, aux_values, reliability_mask, unc_w1, unc_b1, unc_w2, unc_b2, gate_w1, gate_bias):
        import math
        import jax, jax.numpy as jnp
        import numpy as np
        B, S, H, BOT, RD, N, K = (4, 1024, 512, 128, 48, 2048, 8)
        query = jnp.einsum('bsh,dh->bsd', hidden_states, q_proj_w)
        rq = jnp.einsum('bsd,rd->bsr', query, router_w)
        rk = jnp.einsum('nd,rd->nr', aux_keys, router_w)
        scores = jnp.einsum('bsr,nr->bsn', rq, rk) / math.sqrt(RD)
        scores = scores + reliability_mask[None, None, :]
        top_scores, top_idx = jax.lax.top_k(scores, K)
        mean = hidden_states.mean(axis=-1, keepdims=True)
        variance = ((hidden_states - mean) ** 2).mean(axis=-1)
        log_var = jnp.log1p(variance)
        normalized_var = log_var / (log_var.mean() + 1e-06)
        h1 = jax.nn.gelu(jnp.einsum('bsh,fh->bsf', hidden_states, unc_w1) + unc_b1, approximate=False)
        learned = (jnp.einsum('bsf,of->bso', h1, unc_w2) + unc_b2)[..., 0]
        uncertainty = jnp.clip(normalized_var * 0.5 + jax.nn.sigmoid(learned) * 2.5, 0.0, 5.0)
        gate = jax.nn.sigmoid(gate_w1 * uncertainty + gate_bias)
        w = jax.nn.softmax(top_scores, axis=-1)
        v = aux_values[top_idx]
        agg = jnp.einsum('bsk,bskh->bsh', w, v)
        out = hidden_states + gate[..., None] * agg
        return out
    x = x + _L0_attn_ref(_layernorm(x, axis=-1), L0_attn_Wq, L0_attn_Wk, L0_attn_Wv, L0_attn_Wff, L0_attn_bff)
    x = x + _L0_xattn_ref(ctx_1024, ctx_1024, _layernorm(x, axis=-1), L0_xattn_Wk, L0_xattn_Wv, L0_xattn_bv, L0_xattn_Wq, L0_xattn_bq, L0_xattn_Wo, L0_xattn_bo)
    x = x + _L0_ffn_ref(_layernorm(x, axis=-1), L0_ffn_q_proj_w, L0_ffn_router_w, L0_ffn_aux_keys, L0_ffn_aux_values, L0_ffn_reliability_mask, L0_ffn_unc_w1, L0_ffn_unc_b1, L0_ffn_unc_w2, L0_ffn_unc_b2, L0_ffn_gate_w1, L0_ffn_gate_bias)
    return x

_drawn_inputs = setup_inputs


def setup_inputs(seed=0):
    import zlib

    import numpy as np

    out = dict(_drawn_inputs(seed))
    spreads = {'L0_xattn_bv': (0.0, 0.1),
     'L0_xattn_bq': (0.0, 0.45),
     'L0_xattn_bo': (0.0, 0.1),
     'L0_ffn_unc_b1': (0.0, 0.8)}
    factors = {'L0_attn_Wq': 3.088,
     'L0_attn_Wk': 3.016,
     'L0_attn_bff': 6.089,
     'L0_ffn_q_proj_w': 8.0,
     'L0_ffn_router_w': 8.0,
     'L0_ffn_aux_keys': 8.0,
     'L0_ffn_aux_values': 8.0,
     'L0_ffn_unc_w1': 8.0,
     'L0_ffn_unc_w2': 8.0}
    for name, (base, spread) in spreads.items():
        noise = np.random.default_rng([zlib.crc32(name.encode()), seed]).standard_normal(out[name].shape)
        drawn = base * np.exp(spread * noise) if base else spread * noise
        out[name] = jnp.asarray(drawn.astype(out[name].dtype))
    for name, factor in factors.items():
        out[name] = (out[name] * factor).astype(out[name].dtype)
    return out
```

```python
from contextlib import ExitStack

import concourse.bass as bass
from concourse import mybir

F32 = mybir.dt.float32
I32 = mybir.dt.int32
U32 = mybir.dt.uint32
ALU = mybir.AluOpType
ACT = mybir.ActivationFunctionType
AX_X = mybir.AxisListType.X
AX_XY = mybir.AxisListType.XY

P = 128
B, S, D = 32, 224, 512
C = D // P
T, R = 2, S // 2
H = 16
DH = D // H
HB = P // DH
NB = H // HB
UNITS = NB * T
SK = 750
KC = 6
KP = SK // KC
HK = SK // 2
N, K8, RD = 2048, 8, 48
BOT = 128
BANK = 512
EPS = 1e-5
RSQRT_SEED = 1597463007.0

A_BANKS, X_BANKS, F_BANKS = 4, 2, 2
A_JOBS, X_JOBS, F_JOBS = 52, 24, 12

A_XT, A_QK, A_V, A_OT, A_FF = 0, 2, 6, 48, 50


def a_scores(u):
    return 8 + 2 * u if u < 2 else 14 + 5 * (u - 2)


def a_probs(u):
    return (12, 16, 21, 26, 31, 36, 41, 44)[u]


def a_mixed(u):
    return (18, 23, 28, 33, 38, 43, 46, 47)[u]


X_C0, X_XT, X_C1, X_G, X_S, X_P, X_U, X_M = 0, 4, 6, 10, 12, 16, 20, 22
F_XT, F_R, F_L, F_S = 0, 2, 3, 4

ORDER = (
    ("X", "norm", 0), ("F", "norm", 0), ("X", "ctx", 0), ("A", "norm", 0), ("X", "turn", 0),
    ("X", "ctx", 1), ("F", "turn", 0), ("X", "query", 0), ("G", "sum", 0), ("A", "turn", 0),
    ("F", "route", 0), ("A", "qk", 0), ("X", "score", 0), ("A", "value", 0), ("X", "score", 1),
    ("A", "score", 0), ("X", "prob", 0), ("A", "unit", 0), ("X", "prob", 1), ("A", "unit", 1),
    ("X", "mix", 0), ("A", "unit", 2), ("F", "learn", 0), ("A", "unit", 3), ("F", "score", 0),
    ("X", "out", 0), ("A", "unit", 4), ("F", "top", 0), ("A", "unit", 5), ("G", "sum", 1),
    ("A", "unit", 6), ("F", "score", 1), ("A", "unit", 7), ("A", "unit", 8), ("F", "top", 1),
    ("A", "turn_out", 0), ("A", "out", 0),
)

A_STEPS, X_STEPS, F_STEPS, G_STEPS = 21, 15, 18, 18


def build(nc, x, ctx, attn_wq, attn_wk, attn_wv, attn_wff, attn_bff, x_wk, x_wv, x_bv, x_wq, x_bq,
          x_wo, x_bo, q_proj_w, router_w, aux_keys, aux_values, mask, unc_w1, unc_b1, unc_w2,
          unc_b2, gate_w1, gate_bias, out):
    stack = ExitStack()
    with stack:
        def sb(name, shape, dt=F32):
            return stack.enter_context(nc.sbuf_tensor(name, shape, dt))

        def sem(name):
            return stack.enter_context(nc.semaphore(name))

        base_dram = nc.dram_tensor("base_scratch", [B, S, D], F32).ap()
        agg_dram = nc.dram_tensor("agg_scratch", [B, S, D], F32).ap()

        wqT, wkT, wvT, wffT, m1, m2 = (
            sb(n, [P, C, D]) for n in ("wqT", "wkT", "wvT", "wffT", "m1", "m2"))
        rkT = sb("rkT", [RD + 1, N])
        routeT = sb("routeT", [P, C, RD])
        unc1T = sb("unc1T", [P, C, BOT])
        rwT = sb("rwT", [P, RD])
        ident = sb("ident", [P, P])
        ones = sb("ones", [P, P])
        qmask = sb("qmask", [P, HB])
        bff = sb("bff", [R, D])
        cb = sb("cb", [R, D])
        bvc, bqc, gb = (sb(n, [P, C]) for n in ("bvc", "bqc", "gb"))
        b1c, w2c = sb("b1c", [P, 1]), sb("w2c", [P, 1])
        b2c, gwc, gbc = (sb(n, [R, 1]) for n in ("b2c", "gwc", "gbc"))

        xa = sb("xa", [R, T, D])
        xna = sb("xna", [R, T, D])
        xnaT = sb("xnaT", [P, C, S])
        qm = sb("qm", [P, NB, HB, S])
        kT = sb("kT", [P, NB, S])
        va = sb("va", [R, T, H, DH + 1])
        pa = sb("pa", [R, 2, HB, S])
        paT = sb("paT", [R, 2, T, HB, R])
        oa = sb("oa", [R, T, H, DH])
        nmax = sb("nmax", [R, 2, HB])
        rsum = sb("rsum", [R, UNITS, HB])
        x1 = sb("x1", [R, T, D])
        xnx = sb("xnx", [R, T, D])
        xnxT = sb("xnxT", [P, C, S])
        gT = sb("gT", [P, C, S])
        cx = sb("cx", [P, KC * D])
        cxT = sb("cxT", [P, C * SK])
        px = sb("px", [R, T, SK])
        pxT = sb("pxT", [KP, KC, S])
        uT = xnxT
        xmax = sb("xmax", [R, T])
        xsum = sb("xsum", [R, T, 2])
        xrec = sb("xrec", [R, T])
        x2 = sb("x2", [R, T, D])
        xnf = sb("xnf", [R, T, D])
        xnfT = sb("xnfT", [P, C, S])
        rqT = sb("rqT", [RD + 1, S])
        h1 = sb("h1", [BOT, S])
        sc = sb("sc", [P, N])
        top = sb("top", [R, T, K8])
        ntop = sb("ntop", [R, T])
        idx = sb("idx", [R, T, K8], U32)
        wt = sb("wt", [R, T, K8])
        wsum = sb("wsum", [R, T])
        vg = sb("vg", [P, K8 * D])
        agg = sb("agg", [R, D])
        stats = {s: sb(f"stats_{s}", [R, T, 6]) for s in "AXF"}
        mv = {s: sb(f"mv_{s}", [R, T, 2]) for s in "AXF"}
        ve = {s: sb(f"ve_{s}", [R, T]) for s in "AXF"}
        rstd = {s: sb(f"rstd_{s}", [R, T]) for s in "AXF"}
        tmp = {s: sb(f"tmp_{s}", [R, T]) for s in "AXF"}
        var_all = sb("var_all", [R, B * T])
        gate = sb("gate", [R, B * T])
        lsum = sb("lsum", [R, 1])
        rmean = sb("rmean", [R, 1])

        cxv = cx[0:KP, :].rearrange("p (j d) -> p j d", j=KC)
        cxTv = cxT[:, :].rearrange("p (c k) -> p c k", c=C)
        vgv = vg[0:R, :].rearrange("p (k d) -> p k d", k=K8)

        psA = stack.enter_context(nc.psum_tensor("psA", [P, A_BANKS, BANK], F32))
        psX = stack.enter_context(nc.psum_tensor("psX", [P, X_BANKS, BANK], F32))
        psF = stack.enter_context(nc.psum_tensor("psF", [P, F_BANKS, BANK], F32))
        ps = {"A": psA, "X": psX, "F": psF}
        banks = {"A": A_BANKS, "X": X_BANKS, "F": F_BANKS}
        jobs = {"A": A_JOBS, "X": X_JOBS, "F": F_JOBS}
        full = {s: [sem(f"{s}_full{k}") for k in range(n)] for s, n in banks.items()}
        drained = {s: [sem(f"{s}_drained{k}") for k in range(n)] for s, n in banks.items()}

        setup_loaded = [sem(f"setup_loaded{k}") for k in range(4)]
        setup_full, setup_drained = sem("setup_full"), sem("setup_drained")
        const_step, const_ready = sem("const_step"), sem("const_ready")
        small_step = sem("small_step")
        waited = sem("waited")
        x_loaded, ctx_loaded = sem("x_loaded"), sem("ctx_loaded")
        xa_normed, xa_biased = sem("xa_normed"), sem("xa_biased")
        x1_normed, x1_biased = sem("x1_normed"), sem("x1_biased")
        x2_normed, base_ready, base_stored = sem("x2_normed"), sem("base_ready"), sem("base_stored")
        a_maxed, x_maxed = sem("a_maxed"), sem("x_maxed")
        sc_searched, top_ready, top_exped = sem("sc_searched"), sem("top_ready"), sem("top_exped")
        gathered, agg_ready, agg_stored = sem("gathered"), sem("agg_ready"), sem("agg_stored")
        steps = {s: sem(f"dve_step_{s}") for s in "AXFG"}
        log_done, mean_full = sem("log_done"), sem("mean_full")
        tail_step, gate_ready = sem("tail_step"), sem("gate_ready")
        logit_done, clip_ready = sem("logit_done"), sem("clip_ready")

        def wait(eng, s, value):
            if not (isinstance(value, int) and value <= 0):
                eng.wait_ge(s, value)

        def apart(eng):
            eng.sem_inc(waited, 1)

        def bank(s, j):
            return ps[s][:, j % banks[s], :]

        def nth(s, j, b):
            return jobs[s] // banks[s] * b + j // banks[s]

        def wait_free(eng, s, j, b):
            wait(eng, drained[s][j % banks[s]], nth(s, j, b))

        def wait_full(eng, s, j, b):
            wait(eng, full[s][j % banks[s]], nth(s, j, b) + 1)

        def wait_drained(eng, s, j, b):
            wait(eng, drained[s][j % banks[s]], nth(s, j, b) + 1)

        def pipeline(eng, step):
            def iteration(i):
                batch = {"A": i, "X": i - 1, "F": i - 2, "G": i - 3}
                for s, name, arg in ORDER:
                    b = batch[s]
                    outside = isinstance(b, int) and not 0 <= b < B
                    if (s, name) in step and not outside:
                        step[s, name](b, arg)

            for i in range(3):
                iteration(i)
            with eng.Fori(3, B - 1) as i:
                iteration(i)
            for i in range(B - 1, B + 3):
                iteration(i)

        def row(t, b):
            return t[b, :, :] if isinstance(b, int) else t[bass.ds(b, 1), :, :].rearrange("a s d -> (a s) d")

        def tiles(a):
            return a.rearrange("(t r) d -> r t d", r=R)

        def columns(a, b):
            return a[:, T * b:T * b + T] if isinstance(b, int) else a[:, bass.ds(T * b, T)]

        stage = [cx[:, 0:C * D], vg[:, 0:C * D], vg[:, C * D:2 * C * D], sc[:, :]]
        st = [a.rearrange("p (c d) -> p c d", c=C) for a in stage]
        woT = cxT[:, 0:C * D].rearrange("p (c d) -> p c d", c=C)
        keysT = cxT[:, 0:N]
        keys = st[0].rearrange("p c (a d) -> p (c a) d", d=BOT)
        qw, uw1, rw = stage[1][:, 0:D], stage[1][:, D:2 * D], stage[1][0:RD, 2 * D:2 * D + BOT]
        ROUND1, ROUND2, ROUND3 = 16, 16 + 4 + 4 + 1 + 4 + 1, 30 + 1 + 1 + 4 + 4 + 1
        SMALL = 10
        bv_rows = uT[:, :, 0:R]

        ring = [(w[0:R, 0:T, :], w[0:R, T:2 * T, :]) for w in (wqT, wkT, wvT, wffT)]
        RING = len(ring)
        tail_loaded = [sem(f"tail_loaded{k}") for k in range(RING)]
        tail_added = [sem(f"tail_added{k}") for k in range(RING)]
        tail_stored = [sem(f"tail_stored{k}") for k in range(RING)]

        block = stack.enter_context(nc.Block())

        @block.sync
        def _(sp):
            def rows(w):
                return w.rearrange("(c p) d -> p c d", p=P)

            def small(dst, src):
                sp.dma_start(dst, src).then_inc(setup_loaded[3], 16)

            for k, w in enumerate((attn_wq, attn_wk, attn_wv, attn_wff)):
                sp.dma_start(st[k], rows(w)).then_inc(setup_loaded[0], 16)
            with nc.allow_non_contiguous_dma(reason="bias columns, once"):
                small(bvc[:, :], x_bv.rearrange("(c p) -> p c", p=P))
                small(bqc[:, :], x_bq.rearrange("(c p) -> p c", p=P))
                small(b1c[:, :], unc_b1.rearrange("(p a) -> p a", a=1))
                small(w2c[:, :], unc_w2.rearrange("a p -> p a"))
            small(bff[:, :], attn_bff.partition_broadcast(R))
            small(cb[:, :], x_bo.partition_broadcast(R))
            small(b2c[:, :], unc_b2.partition_broadcast(R))
            small(gwc[:, :], gate_w1.partition_broadcast(R))
            small(gbc[:, :], gate_bias.partition_broadcast(R))
            small(rkT[RD:RD + 1, :], mask.rearrange("(a n) -> a n", a=1))
            sp.dma_start(xa[:, :, :], tiles(row(x, 0))).then_inc(x_loaded, 16)
            sp.wait_ge(setup_drained, ROUND1)
            for k, w in enumerate((x_wo, x_wv, x_wq, x_wk)):
                sp.dma_start(st[k], rows(w)).then_inc(setup_loaded[1], 16)
            sp.wait_ge(setup_drained, ROUND2)
            sp.dma_start(keys, aux_keys.rearrange("(c p) d -> p c d", p=P)).then_inc(setup_loaded[2], 16)
            sp.dma_start(qw, q_proj_w).then_inc(setup_loaded[2], 16)
            sp.dma_start(uw1, unc_w1).then_inc(setup_loaded[2], 16)
            sp.dma_start(rw, router_w).then_inc(setup_loaded[2], 16)
            sp.wait_ge(setup_drained, ROUND3)
            sp.dma_start(cxv, row(ctx, 0).rearrange("(p j) d -> p j d", j=KC)).then_inc(ctx_loaded, 16)

            def next_ctx(b, _):
                if isinstance(b, int) and b == B - 1:
                    return
                wait_full(sp, "X", X_U + 1, b)
                sp.dma_start(cxv, row(ctx, b + 1).rearrange("(p j) d -> p j d", j=KC)).then_inc(ctx_loaded, 16)

            def next_x(b, _):
                if isinstance(b, int) and b == B - 1:
                    return
                wait_drained(sp, "A", A_FF + 1, b)
                sp.dma_start(xa[:, :, :], tiles(row(x, b + 1))).then_inc(x_loaded, 16)

            def store_base(b, _):
                sp.wait_ge(base_ready, b + 1)
                sp.dma_start(tiles(row(base_dram, b)), x2[:, :, :]).then_inc(base_stored, 16)

            def store_agg(b, t):
                sp.wait_ge(agg_ready, T * b + t + 1)
                sp.dma_start(tiles(row(agg_dram, b))[:, t, :], agg[:, :]).then_inc(agg_stored, 16)

            pipeline(sp, {("X", "mix"): next_ctx, ("A", "out"): next_x, ("F", "norm"): store_base,
                          ("G", "sum"): store_agg})

            sp.wait_ge(base_stored, 16 * B)
            sp.wait_ge(agg_stored, 16 * T * B)

            def reload(q):
                for k, (base_t, agg_t) in enumerate(ring):
                    wait(sp, tail_stored[k], 16 * q)
                    sp.dma_start(base_t, tiles(row(base_dram, RING * q + k))).then_inc(tail_loaded[k], 16)
                    sp.dma_start(agg_t, tiles(row(agg_dram, RING * q + k))).then_inc(tail_loaded[k], 16)

            reload(0)
            with sp.Fori(1, B // RING) as q:
                reload(q)

        @block.gpsimd
        def _(pool):
            nc.gpsimd.memset(ident[:, :], 0.0).then_inc(const_step, 1)
            nc.gpsimd.memset(qmask[:, :], float(D) ** -0.5).then_inc(const_step, 1)
            nc.gpsimd.memset(ones[:, :], 1.0)
            nc.gpsimd.memset(va[:, :, :, :], 1.0)
            nc.gpsimd.memset(rqT[:, :], 1.0)
            pool.wait_ge(const_step, 2)
            nc.gpsimd.affine_select(out=ident[:, :], in_=ident[:, :], compare_op=ALU.not_equal, fill=1.0,
                                    base=0, pattern=[[-1, P]], channel_multiplier=1)
            nc.gpsimd.affine_select(out=qmask[:, :], in_=qmask[:, :], compare_op=ALU.is_ge, fill=0.0,
                                    base=0, pattern=[[-DH, HB]], channel_multiplier=1).then_inc(const_step, 1)
            pool.wait_ge(const_step, 3)
            nc.gpsimd.affine_select(out=qmask[:, :], in_=qmask[:, :], compare_op=ALU.is_ge, fill=0.0,
                                    base=DH - 1, pattern=[[DH, HB]], channel_multiplier=-1).then_inc(const_ready, 1)

            def bias_x(b, _):
                pool.wait_ge(xa_normed, b + 1)
                nc.gpsimd.tensor_tensor(xa[:, :, :], xa[:, :, :], bff[:, :].unsqueeze(1).to_broadcast([R, T, D]),
                                        ALU.add).then_inc(xa_biased, 1)

            def bias_x1(b, _):
                pool.wait_ge(x1_normed, b + 1)
                nc.gpsimd.tensor_tensor(x1[:, :, :], x1[:, :, :], cb[:, :].unsqueeze(1).to_broadcast([R, T, D]),
                                        ALU.add).then_inc(x1_biased, 1)

            def add_base(b, _):
                pool.wait_ge(x2_normed, b + 1)
                nc.gpsimd.tensor_tensor(x2[:, :, :], x2[:, :, :], xnf[:, :, :], ALU.add).then_inc(base_ready, 1)

            def gather(b, t):
                pool.wait_ge(sc_searched, T * b + t + 1)
                wait(pool, agg_ready, T * b + t)
                apart(pool)
                for k in range(K8):
                    pool.indirect_dma_start(vgv[:, k, :], None, aux_values,
                                            bass.IndirectOffsetOnAxis(ap=idx[:, t, k:k + 1], axis=0)).then_inc(gathered, 16)

            pool.wait_ge(setup_loaded[3], 16 * SMALL)
            pool.wait_ge(setup_drained, ROUND3)
            pipeline(pool, {("A", "norm"): bias_x, ("X", "norm"): bias_x1, ("F", "norm"): add_base,
                            ("G", "sum"): lambda b, t: gather(b, 1) if t == 0 else None,
                            ("F", "top"): lambda b, t: gather(b, 0) if t == 0 else None})

        @block.scalar
        def _(act):
            def copy_out(s, j, b, dst, src):
                wait_full(act, s, j, b)
                nc.scalar.copy(dst, src).then_inc(drained[s][j % banks[s]], 1)

            def turn(s, first, dst):
                def step(b, _):
                    for j in range(2):
                        copy_out(s, first + j, b, dst[:, 2 * j:2 * j + 2, :],
                                 bank(s, first + j)[:, 0:2 * S].rearrange("p (c s) -> p c s", c=2))
                return step

            def value(b, _):
                for t in range(T):
                    copy_out("A", A_V + t, b, va[:, t, :, 0:DH],
                             bank("A", A_V + t)[0:R, :].rearrange("p (h d) -> p h d", h=H))

            def exp_scores(b, u):
                if u >= 2:
                    wait_full(act, "A", a_probs(u - 2) + 1, b)
                for j in range(2):
                    job = a_scores(u) + j
                    act.wait_ge(a_maxed, 2 * UNITS * b + 2 * u + j + 1)
                    for h in (2 * j, 2 * j + 1):
                        last = nc.scalar.activation(pa[:, u % 2, h, :], bank("A", job)[0:R, (h % 2) * S:(h % 2 + 1) * S],
                                                    ACT.Exp, bias=nmax[:, u % 2, h:h + 1])
                    last.then_inc(drained["A"][job % A_BANKS], 1)

            def unit(b, u):
                if u + 1 < UNITS:
                    exp_scores(b, u + 1)

            def ctx_turned(b, part):
                for q in (4 * part, 4 * part + 2):
                    j = (X_C0 if part == 0 else X_C1) + q % 4
                    copy_out("X", j, b, cxTv[:, q // 2, 0:HK], bank("X", j)[:, 0:HK])

            def query(b, _):
                for j in range(2):
                    wait_full(act, "X", X_G + j, b)
                    for k in range(2):
                        c = 2 * j + k
                        last = nc.scalar.activation(gT[:, c, :], bank("X", X_G + j)[:, k * S:(k + 1) * S],
                                                    ACT.Identity, bias=gb[:, c:c + 1])
                    last.then_inc(drained["X"][(X_G + j) % X_BANKS], 1)

            def x_exp(b, t):
                act.wait_ge(x_maxed, T * b + t + 1)
                for j in range(2):
                    job = X_S + 2 * t + j
                    nc.scalar.activation(px[:, t, j * HK:(j + 1) * HK], bank("X", job)[0:R, 0:HK], ACT.Exp,
                                         bias=xmax[:, t:t + 1], accum_out=xsum[:, t, j:j + 1])\
                        .then_inc(drained["X"][job % X_BANKS], 1)

            def route(b, _):
                wait_full(act, "F", F_R, b)
                nc.scalar.copy(rqT[0:RD, :], bank("F", F_R)[0:RD, 0:S])
                nc.scalar.activation(h1[:, :], bank("F", F_R)[:, S:2 * S], ACT.Gelu, bias=b1c[:, 0:1])\
                    .then_inc(drained["F"][F_R % F_BANKS], 1)

            def f_score(b, t):
                wait(act, sc_searched, T * b + t)
                for n in range(4):
                    j = F_S + 4 * t + n
                    copy_out("F", j, b, sc[0:R, n * BANK:(n + 1) * BANK], bank("F", j)[0:R, :])

            def f_top(b, t):
                act.wait_ge(top_ready, T * b + t + 1)
                wait(act, agg_ready, T * (b - 1) + t + 1)
                nc.scalar.activation(wt[:, t, :], top[:, t, :], ACT.Exp, bias=ntop[:, t:t + 1],
                                     accum_out=wsum[:, t:t + 1]).then_inc(top_exped, 1)

            act.wait_ge(setup_loaded[3], 16 * SMALL)
            act.wait_ge(setup_drained, ROUND3)
            act.wait_ge(const_ready, 1)
            pipeline(act, {("A", "turn"): turn("A", A_XT, xnaT), ("A", "turn_out"): turn("A", A_OT, xnaT),
                           ("X", "turn"): turn("X", X_XT, xnxT), ("X", "mix"): turn("X", X_U, uT),
                           ("F", "turn"): turn("F", F_XT, xnfT), ("A", "value"): value,
                           ("A", "score"): exp_scores, ("A", "unit"): unit, ("X", "ctx"): ctx_turned,
                           ("X", "query"): query, ("X", "score"): x_exp, ("F", "route"): route,
                           ("F", "score"): f_score, ("F", "top"): f_top})

            act.wait_ge(steps["F"], F_STEPS * B)
            nc.scalar.activation(var_all[:, :], var_all[:, :], ACT.Ln, bias=1.0, accum_out=lsum[:, :])\
                .then_inc(log_done, 1)
            wait_drained(act, "F", F_L, B - 1)
            nc.scalar.activation(gate[:, :], gate[:, :], ACT.Sigmoid, bias=b2c[:, 0:1]).then_inc(logit_done, 1)
            act.wait_ge(tail_step, 4)
            nc.scalar.activation(gate[:, :], gate[:, :], ACT.Sigmoid, scale=gwc[:, 0:1], bias=gbc[:, 0:1])\
                .then_inc(gate_ready, 1)
            with act.Fori(0, B // RING) as q:
                for k, (base_t, _) in enumerate(ring):
                    act.wait_ge(tail_added[k], q + 1)
                    act.dma_start(tiles(row(out, RING * q + k)), base_t).then_inc(tail_stored[k], 16)
            for k in range(RING):
                act.wait_ge(tail_stored[k], 16 * (B // RING))

        @block.vector
        def _(dve):
            count = {}

            def mark(s, ins):
                ins.then_inc(steps[s], 1)
                count[s] += 1

            def settle(s, b):
                dve.wait_ge(steps[s], per_batch[s] * b + count[s])

            per_batch = {"A": A_STEPS, "X": X_STEPS, "F": F_STEPS, "G": G_STEPS}

            def norm(s, b, src, dst, normed):
                count[s] = 0
                for t in range(T):
                    last = nc.vector.bn_stats(stats[s][:, t, :], src[:, t, :])
                mark(s, last)
                settle(s, b)
                apart(dve)
                for t in range(T):
                    last = nc.vector.bn_aggr(mv[s][:, t, :], stats[s][:, t, :])
                mark(s, last)
                settle(s, b)
                mark(s, nc.vector.tensor_scalar(ve[s][:, :], mv[s][:, :, 1], EPS, None, ALU.add))
                settle(s, b)
                mark(s, nc.vector.tensor_scalar(rstd[s][:, :].bitcast(I32), ve[s][:, :].bitcast(I32), -0.5, RSQRT_SEED,
                                                ALU.mult, ALU.add))
                for _ in range(3):
                    settle(s, b)
                    mark(s, nc.vector.scalar_tensor_tensor(tmp[s][:, :], rstd[s][:, :], -0.5, ve[s][:, :], ALU.mult, ALU.mult))
                    settle(s, b)
                    mark(s, nc.vector.tensor_tensor(tmp[s][:, :], tmp[s][:, :], rstd[s][:, :], ALU.mult))
                    settle(s, b)
                    mark(s, nc.vector.scalar_tensor_tensor(rstd[s][:, :], tmp[s][:, :], 1.5, rstd[s][:, :], ALU.add, ALU.mult))
                settle(s, b)
                for t in range(T):
                    last = nc.vector.tensor_scalar(dst[:, t, :], src[:, t, :], mv[s][:, t, 0:1], rstd[s][:, t:t + 1],
                                                   ALU.subtract, ALU.mult)
                last.then_inc(normed, 1)

            def a_norm(b, _):
                dve.wait_ge(x_loaded, 16 * (b + 1))
                wait_full(dve, "A", A_XT + 1, b - 1)
                norm("A", b, xa, xna, xa_normed)

            def x_norm(b, _):
                wait_drained(dve, "A", A_FF, b)
                wait_drained(dve, "A", A_FF + 1, b)
                wait_full(dve, "X", X_XT + 1, b - 1)
                norm("X", b, x1, xnx, x1_normed)

            def f_norm(b, _):
                wait_drained(dve, "X", X_M, b)
                wait_drained(dve, "X", X_M + 1, b)
                wait_full(dve, "F", F_XT + 1, b - 1)
                wait(dve, base_ready, b)
                norm("F", b, x2, xnf, x2_normed)
                dve.wait_ge(x2_normed, b + 1)
                for t in range(T):
                    last = nc.vector.bn_stats(stats["F"][:, t, :], xnf[:, t, :])
                mark("F", last)
                settle("F", b)
                apart(dve)
                for t in range(T):
                    last = nc.vector.bn_aggr(mv["F"][:, t, :], stats["F"][:, t, :])
                mark("F", last)
                settle("F", b)
                mark("F", nc.vector.tensor_copy(columns(var_all, b), mv["F"][:, :, 1]))

            def qk(b, _):
                for k in range(NB):
                    j = A_QK + k
                    wait_full(dve, "A", j, b)
                    nc.vector.tensor_tensor(qm[:, k, :, :], bank("A", j)[:, 0:S].unsqueeze(1).to_broadcast([P, HB, S]),
                                            qmask[:, :].unsqueeze(2).to_broadcast([P, HB, S]), ALU.mult)
                    nc.vector.tensor_copy(kT[:, k, :], bank("A", j)[:, S:2 * S]).then_inc(drained["A"][j % A_BANKS], 1)

            def maxima(b, u):
                for j in range(2):
                    job = a_scores(u) + j
                    wait_full(dve, "A", job, b)
                    nc.vector.tensor_reduce(nmax[:, u % 2, 2 * j:2 * j + 2],
                                            bank("A", job)[0:R, 0:2 * S].rearrange("p (h s) -> p h s", h=2),
                                            AX_X, ALU.max, negate=True).then_inc(a_maxed, 1)

            def probs_turned(b, u):
                for t in range(T):
                    j = a_probs(u) + t
                    wait_full(dve, "A", j, b)
                    nc.vector.tensor_copy(paT[:, u % 2, t, :, :], bank("A", j)[0:R, 0:HB * R].rearrange("p (h q) -> p h q", h=HB))\
                        .then_inc(drained["A"][j % A_BANKS], 1)

            def mixed(b, u):
                k, t = divmod(u, T)
                j = a_mixed(u)
                wait_full(dve, "A", j, b)
                src = bank("A", j)[0:R, 0:HB * (DH + 1)].rearrange("p (h d) -> p h d", h=HB)
                mark("A", nc.vector.reciprocal(rsum[:, u, :], src[:, :, DH]))
                settle("A", b)
                nc.vector.tensor_tensor(oa[:, t, HB * k:HB * (k + 1), :], src[:, :, 0:DH],
                                        rsum[:, u, :].unsqueeze(2).to_broadcast([R, HB, DH]), ALU.mult)\
                    .then_inc(drained["A"][j % A_BANKS], 1)

            def unit(b, u):
                if u + 1 < UNITS:
                    maxima(b, u + 1)
                if u < UNITS:
                    probs_turned(b, u)
                if u >= 1:
                    mixed(b, u - 1)

            def a_out(b, _):
                assert count["A"] == A_STEPS
                dve.wait_ge(xa_biased, b + 1)
                for t in range(T):
                    j = A_FF + t
                    wait_full(dve, "A", j, b)
                    nc.vector.tensor_tensor(x1[:, t, :], bank("A", j)[0:R, :], xa[:, t, :], ALU.add)\
                        .then_inc(drained["A"][j % A_BANKS], 1)

            def ctx_turned(b, part):
                for q in (4 * part + 1, 4 * part + 3):
                    j = (X_C0 if part == 0 else X_C1) + q % 4
                    wait_full(dve, "X", j, b)
                    nc.vector.tensor_copy(cxTv[:, q // 2, HK:SK], bank("X", j)[:, 0:HK]).then_inc(drained["X"][j % X_BANKS], 1)

            def x_maxima(b, t):
                for j in range(2):
                    wait_full(dve, "X", X_S + 2 * t + j, b)
                nc.vector.tensor_reduce(xmax[:, t:t + 1], psX[0:R, :, 0:HK], AX_XY, ALU.max, negate=True).then_inc(x_maxed, 1)

            def x_probs_turned(b, t):
                for j in range(2):
                    job = X_P + 2 * t + j
                    wait_full(dve, "X", job, b)
                    nc.vector.tensor_copy(pxT[:, 3 * j:3 * j + 3, t * R:(t + 1) * R],
                                          bank("X", job)[0:KP, 0:3 * R].rearrange("p (j q) -> p j q", j=3))\
                        .then_inc(drained["X"][job % X_BANKS], 1)

            def x_out(b, _):
                mark("X", nc.vector.tensor_tensor(xrec[:, :], xsum[:, :, 0], xsum[:, :, 1], ALU.add))
                settle("X", b)
                mark("X", nc.vector.reciprocal(xrec[:, :], xrec[:, :]))
                settle("X", b)
                assert count["X"] == X_STEPS
                dve.wait_ge(x1_biased, b + 1)
                wait(dve, base_stored, 16 * b)
                for t in range(T):
                    j = X_M + t
                    wait_full(dve, "X", j, b)
                    nc.vector.scalar_tensor_tensor(x2[:, t, :], bank("X", j)[0:R, :], xrec[:, t:t + 1], x1[:, t, :],
                                                   ALU.mult, ALU.add).then_inc(drained["X"][j % X_BANKS], 1)

            def learn(b, _):
                wait_full(dve, "F", F_L, b)
                nc.vector.tensor_copy(columns(gate, b), bank("F", F_L)[0:R, 0:T]).then_inc(drained["F"][F_L % F_BANKS], 1)

            def f_top(b, t):
                for n in range(4):
                    wait_drained(dve, "F", F_S + 4 * t + n, b)
                apart(dve)
                mark("F", nc.vector.max(top[:, t, :], sc[0:R, :]))
                settle("F", b)
                nc.vector.tensor_scalar(ntop[:, t:t + 1], top[:, t, 0:1], -1.0, None, ALU.mult).then_inc(top_ready, 1)
                nc.vector.max_index(idx[:, t, :], top[:, t, :], sc[0:R, :]).then_inc(sc_searched, 1)
                assert t == 0 or count["F"] == F_STEPS

            def g_sum(b, t):
                if t == 0:
                    count["G"] = 0
                dve.wait_ge(top_exped, T * b + t + 1)
                mark("G", nc.vector.reciprocal(wsum[:, t:t + 1], wsum[:, t:t + 1]))
                settle("G", b)
                mark("G", nc.vector.tensor_scalar(wt[:, t, :], wt[:, t, :], wsum[:, t:t + 1], None, ALU.mult))
                settle("G", b)
                dve.wait_ge(gathered, 16 * K8 * (T * b + t + 1))
                wait(dve, agg_stored, 16 * (T * b + t))
                mark("G", nc.vector.tensor_scalar(agg[:, :], vgv[:, 0, :], wt[:, t, 0:1], None, ALU.mult))
                for k in range(1, K8):
                    settle("G", b)
                    last = nc.vector.scalar_tensor_tensor(agg[:, :], vgv[:, k, :], wt[:, t, k:k + 1], agg[:, :], ALU.mult, ALU.add)
                    if k < K8 - 1:
                        mark("G", last)
                last.then_inc(agg_ready, 1)
                assert t == 0 or count["G"] == G_STEPS

            fills = [0]

            def made():
                dve.wait_ge(setup_full, fills[0] + 1)
                fills[0] += 1
                return psA[:, (fills[0] - 1) % A_BANKS, :]

            dve.wait_ge(setup_loaded[3], 16 * SMALL)
            nc.vector.tensor_copy(bv_rows, bvc[:, :].unsqueeze(2).to_broadcast([P, C, R])).then_inc(small_step, 1)
            for w in (wqT, wkT, wvT, wffT, woT):
                for c in range(C):
                    nc.vector.tensor_copy(w[:, c, :], made()).then_inc(setup_drained, 1)
            for c in range(C):
                nc.vector.tensor_copy(m2[:, c, :], made()).then_inc(setup_drained, 1)
            nc.vector.tensor_tensor(cb[:, :], made()[0:R, :], cb[:, :], ALU.add).then_inc(setup_drained, 1)
            for c in range(C):
                nc.vector.tensor_scalar(m1[:, c, :], made(), float(D) ** -0.5, None, ALU.mult).then_inc(setup_drained, 1)
            nc.vector.tensor_scalar(gb[:, :], made()[:, 0:C], float(D) ** -0.5, None, ALU.mult).then_inc(setup_drained, 1)
            nc.vector.tensor_copy(rwT[:, :], made()[:, 0:RD]).then_inc(setup_drained, 1)
            nc.vector.tensor_copy(routeT[:, :, :], made()[:, 0:C * RD].rearrange("p (c r) -> p c r", c=C)).then_inc(setup_drained, 1)
            for n in range(4):
                nc.vector.tensor_copy(keysT[:, n * BANK:(n + 1) * BANK], made()).then_inc(setup_drained, 1)
            for n in range(4):
                nc.vector.tensor_scalar(rkT[0:RD, n * BANK:(n + 1) * BANK], made()[0:RD, :], float(RD) ** -0.5, None,
                                        ALU.mult).then_inc(setup_drained, 1)
            nc.vector.tensor_copy(unc1T[:, :, :], made().rearrange("p (c f) -> p c f", c=C)).then_inc(setup_drained, 1)
            assert fills[0] == ROUND3
            dve.wait_ge(const_ready, 1)

            pipeline(dve, {("A", "norm"): a_norm, ("X", "norm"): x_norm, ("F", "norm"): f_norm, ("A", "qk"): qk,
                           ("A", "score"): maxima, ("A", "unit"): unit, ("A", "out"): a_out, ("X", "ctx"): ctx_turned,
                           ("X", "score"): x_maxima, ("X", "prob"): x_probs_turned, ("X", "out"): x_out,
                           ("F", "learn"): learn, ("F", "top"): f_top, ("G", "sum"): g_sum})

            dve.wait_ge(mean_full, 1)
            nc.vector.tensor_scalar(rmean[:, :], bank("F", 0)[0:R, 0:1], 1.0 / (B * S), 1e-6, ALU.mult, ALU.add).then_inc(tail_step, 1)
            dve.wait_ge(tail_step, 1)
            nc.vector.reciprocal(rmean[:, :], rmean[:, :]).then_inc(tail_step, 1)
            dve.wait_ge(tail_step, 2)
            nc.vector.tensor_scalar(var_all[:, :], var_all[:, :], rmean[:, 0:1], 0.5, ALU.mult, ALU.mult).then_inc(tail_step, 1)
            dve.wait_ge(tail_step, 3)
            dve.wait_ge(logit_done, 1)
            nc.vector.scalar_tensor_tensor(gate[:, :], gate[:, :], 2.5, var_all[:, :], ALU.mult, ALU.add).then_inc(clip_ready, 1)
            dve.wait_ge(clip_ready, 1)
            nc.vector.tensor_scalar(gate[:, :], gate[:, :], 0.0, 5.0, ALU.max, ALU.min).then_inc(tail_step, 1)
            dve.wait_ge(gate_ready, 1)
            with dve.Fori(0, B // RING) as q:
                for k, (base_t, agg_t) in enumerate(ring):
                    dve.wait_ge(tail_loaded[k], 32 * q + 32)
                    for t in range(T):
                        col = gate[:, bass.ds(T * RING * q + T * k + t, 1)]
                        last = nc.vector.scalar_tensor_tensor(base_t[:, t, :], agg_t[:, t, :], col, base_t[:, t, :],
                                                              ALU.mult, ALU.add)
                    last.then_inc(tail_added[k], 1)

        @block.tensor
        def _(pe):
            def product(dst, pairs):
                for n, (stationary, moving) in enumerate(pairs):
                    last = nc.tensor.matmul(dst, stationary, moving, start=n == 0, stop=n == len(pairs) - 1)
                return last

            def turned(dst, src):
                k = src.shape[0]
                return nc.tensor.transpose(dst, src, ident[0:k, 0:k])

            def filled(s, j, last):
                last.then_inc(full[s][j % banks[s]], 1)

            def turn(s, first, src):
                def step(b, _):
                    for j in range(2):
                        wait_free(pe, s, first + j, b)
                        for k in range(2):
                            for t in range(T):
                                at = k * S + t * R
                                last = turned(bank(s, first + j)[:, at:at + R],
                                              src[:, t, (2 * j + k) * P:(2 * j + k + 1) * P])
                        filled(s, first + j, last)
                return step

            def after(s, what, step):
                def waited(b, arg):
                    pe.wait_ge(what, b + 1)
                    step(b, arg)
                return waited

            def qk(b, _):
                wait_drained(pe, "A", A_XT + 1, b)
                for k in range(NB):
                    j = A_QK + k
                    wait_free(pe, "A", j, b)
                    for n, w in enumerate((wqT, wkT)):
                        last = product(bank("A", j)[:, n * S:(n + 1) * S],
                                       [(w[:, c, k * P:(k + 1) * P], xnaT[:, c, :]) for c in range(C)])
                    filled("A", j, last)

            def value(b, _):
                for t in range(T):
                    j = A_V + t
                    wait_free(pe, "A", j, b)
                    filled("A", j, product(bank("A", j)[0:R, :],
                                           [(xnaT[:, c, t * R:(t + 1) * R], wvT[:, c, :]) for c in range(C)]))

            def scores(b, u):
                k, t = divmod(u, T)
                if u == 0:
                    wait_drained(pe, "A", A_QK + NB - 1, b)
                for j in range(2):
                    job = a_scores(u) + j
                    wait_free(pe, "A", job, b)
                    for h in range(2):
                        last = product(bank("A", job)[0:R, h * S:(h + 1) * S],
                                       [(qm[:, k, 2 * j + h, t * R:(t + 1) * R], kT[:, k, :])])
                    filled("A", job, last)

            def probs(b, u):
                wait_drained(pe, "A", a_scores(u) + 1, b)
                for t in range(T):
                    j = a_probs(u) + t
                    wait_free(pe, "A", j, b)
                    for h in range(HB):
                        last = turned(bank("A", j)[0:R, h * R:(h + 1) * R], pa[:, u % 2, h, t * R:(t + 1) * R])
                    filled("A", j, last)

            def mixed(b, u):
                k, j = u // T, a_mixed(u)
                wait_drained(pe, "A", a_probs(u) + 1, b)
                if u == 0:
                    wait_drained(pe, "A", A_V + 1, b)
                wait_free(pe, "A", j, b)
                for h in range(HB):
                    last = product(bank("A", j)[0:R, h * (DH + 1):(h + 1) * (DH + 1)],
                                   [(paT[:, u % 2, t, h, :], va[:, t, HB * k + h, :]) for t in range(T)])
                filled("A", j, last)

            def unit(b, u):
                if u + 1 < UNITS:
                    scores(b, u + 1)
                if u < UNITS:
                    probs(b, u)
                if u >= 1:
                    mixed(b, u - 1)

            def turn_out(b, _):
                wait_drained(pe, "A", a_mixed(UNITS - 1), b)
                turn("A", A_OT, oa[:, :, :, :].rearrange("p t h d -> p t (h d)"))(b, _)

            def rows_times(s, first, what, src, w):
                def step(b, _):
                    wait_drained(pe, s, what, b)
                    for t in range(T):
                        wait_free(pe, s, first + t, b)
                        filled(s, first + t, product(bank(s, first + t)[0:R, :],
                                                     [(src[:, c, t * R:(t + 1) * R], w[:, c, :]) for c in range(C)]))
                return step

            def ctx_turn(b, part):
                if part == 0:
                    pe.wait_ge(ctx_loaded, 16 * (b + 1))
                for q in range(4 * part, 4 * part + 4):
                    j = (X_C0 if part == 0 else X_C1) + q % 4
                    wait_free(pe, "X", j, b)
                    for k in range(3):
                        last = turned(bank("X", j)[:, k * KP:(k + 1) * KP],
                                      cxv[:, 3 * (q % 2) + k, (q // 2) * P:(q // 2 + 1) * P])
                    filled("X", j, last)

            def query(b, _):
                wait_drained(pe, "X", X_XT + 1, b)
                for j in range(2):
                    wait_free(pe, "X", X_G + j, b)
                    for k in range(2):
                        i = 2 * j + k
                        last = product(bank("X", X_G + j)[:, k * S:(k + 1) * S],
                                       [(m1[:, c, i * P:(i + 1) * P], xnxT[:, c, :]) for c in range(C)])
                    filled("X", X_G + j, last)

            def x_scores(b, t):
                if t == 0:
                    for j in range(2):
                        wait_drained(pe, "X", X_G + j, b)
                for j in range(2):
                    job = X_S + 2 * t + j
                    wait_free(pe, "X", job, b)
                    filled("X", job, product(bank("X", job)[0:R, 0:HK],
                                             [(gT[:, c, t * R:(t + 1) * R], cxTv[:, c, j * HK:(j + 1) * HK]) for c in range(C)]))

            def x_probs(b, t):
                wait_drained(pe, "X", X_S + 2 * t, b)
                wait_drained(pe, "X", X_S + 2 * t + 1, b)
                for j in range(2):
                    job = X_P + 2 * t + j
                    wait_free(pe, "X", job, b)
                    for k in range(3):
                        n = 3 * j + k
                        last = turned(bank("X", job)[0:KP, k * R:(k + 1) * R], px[:, t, n * KP:(n + 1) * KP])
                    filled("X", job, last)

            def x_mix(b, _):
                for j in range(2):
                    wait_drained(pe, "X", X_P + 2 + j, b)
                for j in range(2):
                    wait_free(pe, "X", X_U + j, b)
                    for k in range(2):
                        i = 2 * j + k
                        last = product(bank("X", X_U + j)[:, k * S:(k + 1) * S],
                                       [(cxv[:, n, i * P:(i + 1) * P], pxT[:, n, :]) for n in range(KC)])
                    filled("X", X_U + j, last)

            def route(b, _):
                wait_drained(pe, "F", F_XT + 1, b)
                wait_free(pe, "F", F_R, b)
                product(bank("F", F_R)[0:RD, 0:S], [(routeT[:, c, :], xnfT[:, c, :]) for c in range(C)])
                filled("F", F_R, product(bank("F", F_R)[:, S:2 * S], [(unc1T[:, c, :], xnfT[:, c, :]) for c in range(C)]))

            def learn(b, _):
                wait_drained(pe, "F", F_R, b)
                wait_free(pe, "F", F_L, b)
                for t in range(T):
                    last = product(bank("F", F_L)[0:R, t:t + 1], [(h1[:, t * R:(t + 1) * R], w2c[:, :])])
                filled("F", F_L, last)

            def f_scores(b, t):
                for n in range(4):
                    j = F_S + 4 * t + n
                    wait_free(pe, "F", j, b)
                    filled("F", j, product(bank("F", j)[0:R, :],
                                           [(rqT[:, t * R:(t + 1) * R], rkT[:, n * BANK:(n + 1) * BANK])]))

            fills = [0]

            def place():
                wait(pe, setup_drained, fills[0] - A_BANKS + 1)
                fills[0] += 1
                return psA[:, (fills[0] - 1) % A_BANKS, :]

            def turn_weight(w):
                for i in range(C):
                    dst = place()
                    for o in range(C):
                        last = turned(dst[:, o * P:(o + 1) * P], w[:, o, i * P:(i + 1) * P])
                    last.then_inc(setup_full, 1)

            pe.wait_ge(const_ready, 1)
            pe.wait_ge(setup_loaded[0], 16 * 4)
            for k in range(4):
                turn_weight(st[k])
            pe.wait_ge(setup_loaded[1], 16 * 4)
            turn_weight(st[0])
            pe.wait_ge(setup_drained, fills[0])
            for i in range(C):
                product(place(), [(st[1][:, e, i * P:(i + 1) * P], woT[:, e, :]) for e in range(C)]).then_inc(setup_full, 1)
            pe.wait_ge(small_step, 1)
            product(place()[0:R, :], [(bv_rows[:, e, :], woT[:, e, :]) for e in range(C)]).then_inc(setup_full, 1)
            for i in range(C):
                product(place(), [(st[2][:, e, i * P:(i + 1) * P], st[3][:, e, :]) for e in range(C)]).then_inc(setup_full, 1)
            dst = place()
            for i in range(C):
                last = product(dst[:, i:i + 1], [(st[3][:, e, i * P:(i + 1) * P], bqc[:, e:e + 1]) for e in range(C)])
            last.then_inc(setup_full, 1)
            pe.wait_ge(setup_loaded[2], 16 * 4)
            turned(place()[:, 0:RD], rw).then_inc(setup_full, 1)
            pe.wait_ge(setup_drained, fills[0])
            dst = place()
            for i in range(C):
                last = product(dst[:, i * RD:(i + 1) * RD], [(qw[:, i * P:(i + 1) * P], rwT[:, :])])
            last.then_inc(setup_full, 1)
            for n in range(4):
                dst = place()
                for k in range(4):
                    last = turned(dst[:, k * P:(k + 1) * P], keys[:, 4 * n + k, :])
                last.then_inc(setup_full, 1)
            pe.wait_ge(setup_drained, fills[0])
            for n in range(4):
                product(place()[0:RD, :], [(rwT[:, :], keysT[:, n * BANK:(n + 1) * BANK])]).then_inc(setup_full, 1)
            dst = place()
            for i in range(C):
                last = turned(dst[:, i * P:(i + 1) * P], uw1[:, i * P:(i + 1) * P])
            last.then_inc(setup_full, 1)
            pe.wait_ge(setup_drained, ROUND3)

            pipeline(pe, {("A", "turn"): after("A", xa_normed, turn("A", A_XT, xna)),
                          ("X", "turn"): after("X", x1_normed, turn("X", X_XT, xnx)),
                          ("F", "turn"): after("F", x2_normed, turn("F", F_XT, xnf)),
                          ("A", "qk"): qk, ("A", "value"): value, ("A", "score"): scores, ("A", "unit"): unit,
                          ("A", "turn_out"): turn_out, ("A", "out"): rows_times("A", A_FF, A_OT + 1, xnaT, wffT),
                          ("X", "ctx"): ctx_turn, ("X", "query"): query, ("X", "score"): x_scores,
                          ("X", "prob"): x_probs, ("X", "mix"): x_mix,
                          ("X", "out"): rows_times("X", X_M, X_U + 1, uT, m2),
                          ("F", "route"): route, ("F", "learn"): learn, ("F", "score"): f_scores})

            pe.wait_ge(log_done, 1)
            wait_free(pe, "F", 0, B)
            product(bank("F", 0)[0:R, 0:1], [(ones[0:R, 0:R], lsum[:, :])]).then_inc(mean_full, 1)


_INS = ['x', 'ctx_1024', 'L0_attn_Wq', 'L0_attn_Wk', 'L0_attn_Wv', 'L0_attn_Wff', 'L0_attn_bff', 'L0_xattn_Wk',
        'L0_xattn_Wv', 'L0_xattn_bv', 'L0_xattn_Wq', 'L0_xattn_bq', 'L0_xattn_Wo', 'L0_xattn_bo',
        'L0_ffn_q_proj_w', 'L0_ffn_router_w', 'L0_ffn_aux_keys', 'L0_ffn_aux_values', 'L0_ffn_reliability_mask',
        'L0_ffn_unc_w1', 'L0_ffn_unc_b1', 'L0_ffn_unc_w2', 'L0_ffn_unc_b2', 'L0_ffn_gate_w1', 'L0_ffn_gate_bias']


def kernel(**inputs):
    import numpy as np
    import concourse.bacc as bacc
    from concourse.bass_utils import run_bass_kernel_spmd

    nc = bacc.Bacc("TRN2", target_bir_lowering=False, num_devices=1)
    arrays, args = {}, []
    for name in _INS:
        a = np.ascontiguousarray(inputs[name])
        if a.ndim == 0:
            a = a.reshape(1)
        arrays[f"in_{name}"] = a
        args.append(nc.dram_tensor(f"in_{name}", a.shape, mybir.dt.from_np(a.dtype), kind="ExternalInput").ap())
    out = nc.dram_tensor("out", [B, S, D], F32, kind="ExternalOutput").ap()
    build(nc, *args, out)
    return run_bass_kernel_spmd(nc, [arrays], core_ids=[0]).results[0]["out"]
```

```python
from contextlib import ExitStack

import concourse.bass as bass
from concourse import mybir

F32 = mybir.dt.float32
F32R = mybir.dt.float32r
I32 = mybir.dt.int32
U32 = mybir.dt.uint32
ALL = slice(None)
ALU = mybir.AluOpType
ACT = mybir.ActivationFunctionType
AX_X = mybir.AxisListType.X
AX_XY = mybir.AxisListType.XY

P = 128
B, S, D = 32, 224, 512
C = D // P
T, R = 2, S // 2
H = 16
DH = D // H
HB = P // DH
NB = H // HB
UNITS = NB * T
SK = 750
KC = 6
KP = SK // KC
HK = SK // 2
N, K8, RD = 2048, 8, 48
BOT = 128
LO = 64
RS = LO + RD
KG = 2
PARTS = K8 // KG
CHUNKS = T * PARTS
BANK = 512
EPS = 1e-5
RSQRT_SEED = 1597463007.0

BANKS = {"A": 4, "X": 2, "F": 2}

ORDER = (
    ("X", "ctx", 0), ("X", "ctx", 1), ("X", "norm", 0), ("X", "turn", 0), ("G", "sum", 0), ("A", "norm", 0),
    ("G", "sum", 1), ("X", "query", 0), ("A", "turn", 0), ("F", "norm", 0), ("A", "qk", 0), ("A", "qk", 1),
    ("F", "turn", 0), ("X", "score", 0), ("A", "score", 0), ("G", "sum", 2), ("A", "score", 1), ("A", "share", 0),
    ("X", "score", 1), ("A", "share", 1), ("A", "prob", 0), ("G", "sum", 3), ("F", "route", 0), ("A", "value", 0),
    ("A", "prob", 1), ("X", "prob", 0), ("A", "score", 2), ("A", "mix", 0), ("G", "sum", 4), ("F", "learn", 0),
    ("A", "mix", 1), ("A", "share", 2), ("X", "prob", 1), ("F", "score", 0), ("A", "prob", 2), ("A", "score", 3),
    ("A", "share", 3), ("A", "qk", 2), ("A", "qk", 3), ("A", "mix", 2), ("A", "score", 4), ("A", "share", 4),
    ("A", "prob", 3), ("X", "mix", 0), ("A", "score", 5), ("F", "top", 0), ("A", "prob", 4), ("A", "share", 5),
    ("X", "mix", 1), ("A", "mix", 3), ("A", "score", 6), ("A", "prob", 5), ("G", "sum", 5), ("A", "share", 6),
    ("X", "out", 0), ("A", "mix", 4), ("A", "score", 7), ("A", "share", 7), ("G", "sum", 6), ("A", "prob", 6),
    ("X", "out", 1), ("A", "mix", 5), ("A", "prob", 7), ("A", "mix", 6), ("A", "mix", 7), ("G", "sum", 7),
    ("F", "score", 1), ("F", "top", 1), ("A", "out", 0),
)

FILLS = {("A", "turn"): 4, ("A", "qk"): 1, ("A", "value"): 2, ("A", "score"): 2, ("A", "prob"): 2,
         ("A", "mix"): 1, ("A", "out"): 2,
         ("X", "ctx"): 4, ("X", "turn"): 2, ("X", "query"): 2, ("X", "score"): 2, ("X", "prob"): 2,
         ("X", "mix"): 1, ("X", "out"): 1,
         ("F", "turn"): 2, ("F", "route"): 1, ("F", "learn"): 1, ("F", "score"): 4}
FILL = {}
JOBS = {"A": 0, "X": 0, "F": 0}
for _s, _step, _arg in ORDER:
    if (_s, _step) in FILLS:
        FILL[_s, _step, _arg] = JOBS[_s]
        JOBS[_s] += FILLS[_s, _step]
assert all(JOBS[_s] % BANKS[_s] == 0 for _s in JOBS)

A_STEPS, X_STEPS, F_STEPS, G_STEPS = 21, 15, 18, 12


def build(nc, x, ctx, attn_wq, attn_wk, attn_wv, attn_wff, attn_bff, x_wk, x_wv, x_bv, x_wq, x_bq,
          x_wo, x_bo, q_proj_w, router_w, aux_keys, aux_values, mask, unc_w1, unc_b1, unc_w2,
          unc_b2, gate_w1, gate_bias, out):
    stack = ExitStack()
    with stack:
        def sb(name, shape, dt=F32):
            return stack.enter_context(nc.sbuf_tensor(name, shape, dt))

        def sem(name):
            return stack.enter_context(nc.semaphore(name))

        base_dram = nc.dram_tensor("base_scratch", [B, S, D], F32).ap()
        agg_dram = nc.dram_tensor("agg_scratch", [B, S, D], F32).ap()

        wqT, wkT, wvT = ((sb(n + "_hi", [P, C, D], F32R), sb(n + "_lo", [P, C, D], F32R)) for n in ("wqT", "wkT", "wvT"))
        wffT = sb("wffT", [P, C, D])
        m1, m2 = sb("m1", [P, C * D]), sb("m2", [P, C * D])
        rkS = sb("rkS", [RS, N], F32R)
        rkL = sb("rkL", [RD + 1, N], F32R)
        routeT = sb("routeT", [P, C, RS])
        unc1T = sb("unc1T", [P, C, BOT])
        ident = sb("ident", [P, P])
        bff = sb("bff", [R, D])
        cb = sb("cb", [R, D])
        bvc, bqc, gb = (sb(n, [P, C]) for n in ("bvc", "bqc", "gb"))
        b1c, w2c = sb("b1c", [P, 1]), sb("w2c", [P, 1])
        b2c, gwc, gbc = (sb(n, [R, 1]) for n in ("b2c", "gwc", "gbc"))

        xa = sb("xa", [R, T, D])
        xo = sb("xo", [R, T, D])
        xT = (sb("xT_hi", [P, C, S], F32R), sb("xT_lo", [P, C, S], F32R))
        qm = (sb("qm_hi", [P, 2, HB, S], F32R), sb("qm_lo", [P, 2, HB, S], F32R))
        kT = (sb("kT_hi", [P, 2, S], F32R), sb("kT_lo", [P, 2, S], F32R))
        va = sb("va", [R, T, H, DH])
        nmax = sb("nmax", [R, 2, HB])
        rsum = sb("rsum", [R, UNITS, HB])
        pa = sb("pa", [R, HB, S])
        oT = sb("oT", [P, C, S])
        big = sb("big", [P, C * SK])
        paT = big[0:R, 0:2 * HB * S].rearrange("p (a t h q) -> p a t h q", a=2, t=T, h=HB)
        cxT = big[:, :].rearrange("p (c k) -> p c k", c=C)
        x1 = sb("x1", [R, T, D])
        nx = sb("nx", [R, T * SK])
        xnx = nx[:, 0:T * D].rearrange("p (t d) -> p t d", t=T)
        xnf = xnx
        px = nx[:, :].rearrange("p (t k) -> p t k", t=T)
        xnxT = sb("xnxT", [P, C, S])
        uT = xnxT
        gT = sb("gT", [P, C, S])
        cx = sb("cx", [P, KC * D])
        cxv = cx[0:KP, :].rearrange("p (j d) -> p j d", j=KC)
        pT = sb("pT", [P, KC, S])
        pxT = pT[0:KP, :, :]
        xnfT = pT[:, 0:C, :]
        xmax = sb("xmax", [R, T])
        xsum = sb("xsum", [R, T, 2])
        xrec = sb("xrec", [R, T])
        x2 = sb("x2", [R, T, D])
        rqS = sb("rqS", [RS, S], F32R)
        sc = sb("sc", [P, N])
        h1 = sc[0:BOT, 0:S]
        top = sb("top", [R, T, K8])
        ntop = sb("ntop", [R, T])
        idx = sb("idx", [R, T, K8], U32)
        wt = sb("wt", [R, T, K8])
        wsum = sb("wsum", [R, T])
        vg = sb("vg", [P, KG * D])
        vgv = vg[0:R, :].rearrange("p (k d) -> p k d", k=KG)
        agg = sb("agg", [R, D])
        stats = {s: sb(f"stats_{s}", [R, T, 6]) for s in "AXF"}
        mv = {s: sb(f"mv_{s}", [R, T, 2]) for s in "AXF"}
        ve = {s: sb(f"ve_{s}", [R, T]) for s in "AXF"}
        rstd = {s: sb(f"rstd_{s}", [R, T]) for s in "AXF"}
        tmp = {s: sb(f"tmp_{s}", [R, T]) for s in "AXF"}
        var_all = sb("var_all", [R, B * T])
        gate = sb("gate", [R, B * T])
        lsum, one = sb("lsum", [R, 1]), sb("one", [R, 1])
        lsums = gT[0:R, 0, 0:R]
        rmean = sb("rmean", [R, 1])

        psA = stack.enter_context(nc.psum_tensor("psA", [P, BANKS["A"], BANK], F32))
        psX = stack.enter_context(nc.psum_tensor("psX", [P, BANKS["X"], BANK], F32))
        psF = stack.enter_context(nc.psum_tensor("psF", [P, BANKS["F"], BANK], F32))
        ps = {"A": psA, "X": psX, "F": psF}
        banks, jobs = BANKS, JOBS
        full = {s: [sem(f"{s}_full{k}") for k in range(n)] for s, n in banks.items()}
        drained = {s: [sem(f"{s}_drained{k}") for k in range(n)] for s, n in banks.items()}

        setup_loaded = [sem(f"setup_loaded{k}") for k in range(5)]
        setup_full, setup_drained = sem("setup_full"), sem("setup_drained")
        const_step, const_ready = sem("const_step"), sem("const_ready")
        small_step, setup_step = sem("small_step"), sem("setup_step")
        waited = sem("waited")
        x_loaded, ctx_loaded = sem("x_loaded"), sem("ctx_loaded")
        xa_normed, xa_biased = sem("xa_normed"), sem("xa_biased")
        x1_normed, x1_biased = sem("x1_normed"), sem("x1_biased")
        x2_normed, base_ready, base_stored = sem("x2_normed"), sem("base_ready"), sem("base_stored")
        a_maxed, a_shared, x_maxed = sem("a_maxed"), sem("a_shared"), sem("x_maxed")
        sc_searched, top_ready, top_exped = sem("sc_searched"), sem("top_ready"), sem("top_exped")
        gathered, summed, agg_stored = sem("gathered"), sem("summed"), sem("agg_stored")
        xT_hi, qk_hi, rq_hi = sem("xT_hi"), sem("qk_hi"), sem("rq_hi")
        small_loaded, mask_loaded = sem("small_loaded"), sem("mask_loaded")
        steps = {s: sem(f"dve_step_{s}") for s in "AXFG"}
        log_done, lsum_spread, mean_full = sem("log_done"), sem("lsum_spread"), sem("mean_full")
        tail_step, gate_ready = sem("tail_step"), sem("gate_ready")
        logit_done, clip_ready = sem("logit_done"), sem("clip_ready")

        def wait(eng, s, value):
            if not (isinstance(value, int) and value <= 0):
                eng.wait_ge(s, value)

        def apart(eng):
            eng.sem_inc(waited, 1)

        def bank(s, j):
            return ps[s][:, j % banks[s], :]

        def nth(s, j, b):
            return jobs[s] // banks[s] * b + j // banks[s]

        def wait_free(eng, s, j, b):
            wait(eng, drained[s][j % banks[s]], nth(s, j, b))

        def wait_full(eng, s, j, b):
            wait(eng, full[s][j % banks[s]], nth(s, j, b) + 1)

        def wait_drained(eng, s, j, b):
            wait(eng, drained[s][j % banks[s]], nth(s, j, b) + 1)

        def pipeline(eng, step):
            def iteration(i):
                batch = {"A": i, "X": i - 1, "F": i - 2, "G": i - 3}
                for s, name, arg in ORDER:
                    b = batch[s]
                    outside = isinstance(b, int) and not 0 <= b < B
                    if (s, name) in step and not outside:
                        step[s, name](b, arg)

            for i in range(3):
                iteration(i)
            with eng.Fori(3, B - 1) as i:
                iteration(i)
            for i in range(B - 1, B + 3):
                iteration(i)

        def row(t, b):
            return t[b, :, :] if isinstance(b, int) else t[bass.ds(b, 1), :, :].rearrange("a s d -> (a s) d")

        def tiles(a):
            return a.rearrange("(t r) d -> r t d", r=R)

        def columns(a, b):
            return a[:, T * b:T * b + T] if isinstance(b, int) else a[:, bass.ds(T * b, T)]

        def weight(a):
            return a[:, 0:C * D].rearrange("p (c d) -> p c d", c=C)

        at_cx, at_m1, at_sc, at_big = weight(cx), weight(m1), weight(sc), weight(big)
        woT = at_big
        keys, keysT = cx[:, 0:N].rearrange("p (c d) -> p c d", d=BOT), big[:, 0:N]
        qw, uw1, rw = sc[:, 0:D], sc[:, D:2 * D], sc[0:RD, 2 * D:2 * D + BOT]
        rk32 = cx[0:RS, 0:N]
        rwT = gT[:, 0, 0:RS]
        bv_rows = uT[:, :, 0:R]
        m1v, m2v = weight(m1), weight(m2)
        WEIGHTS, WO, MIXED = 16, 16 + 4, 20 + 4 + 1 + 4 + 1
        ROUTER, FILLED = MIXED + 1 + 1 + 4 + 4, MIXED + 1 + 1 + 4 + 4 + 1
        READY = FILLED + 2
        SMALL = 9

        ring = [(w[0:R, 0:T * D].rearrange("p (t d) -> p t d", t=T),
                 w[0:R, T * D:2 * T * D].rearrange("p (t d) -> p t d", t=T)) for w in (m1, m2, cx, sc)]
        RING = len(ring)
        tail_loaded = [sem(f"tail_loaded{k}") for k in range(RING)]
        tail_added = [sem(f"tail_added{k}") for k in range(RING)]
        tail_stored = [sem(f"tail_stored{k}") for k in range(RING)]

        block = stack.enter_context(nc.Block())

        @block.sync
        def _(sp):
            def rows(w):
                return w.rearrange("(c p) d -> p c d", p=P)

            def small(dst, src):
                sp.dma_start(dst, src).then_inc(small_loaded, 16)

            for place, w in zip((at_cx, at_m1, at_sc, at_big), (attn_wq, attn_wk, attn_wv, attn_wff)):
                sp.dma_start(place, rows(w)).then_inc(setup_loaded[0], 16)
            with nc.allow_non_contiguous_dma(reason="bias columns, once"):
                small(bvc[:, :], x_bv.rearrange("(c p) -> p c", p=P))
                small(bqc[:, :], x_bq.rearrange("(c p) -> p c", p=P))
                small(b1c[:, :], unc_b1.rearrange("(p a) -> p a", a=1))
                small(w2c[:, :], unc_w2.rearrange("a p -> p a"))
            small(bff[:, :], attn_bff.partition_broadcast(R))
            small(cb[:, :], x_bo.partition_broadcast(R))
            small(b2c[:, :], unc_b2.partition_broadcast(R))
            small(gwc[:, :], gate_w1.partition_broadcast(R))
            small(gbc[:, :], gate_bias.partition_broadcast(R))
            sp.dma_start(xa[:, :, :], tiles(row(x, 0))).then_inc(x_loaded, 16)
            sp.wait_ge(setup_drained, WEIGHTS)
            for place, w in zip((at_cx, at_m1, at_sc), (x_wo, x_wv, x_wq)):
                sp.dma_start(place, rows(w)).then_inc(setup_loaded[1], 16)
            sp.wait_ge(setup_drained, WO)
            sp.dma_start(at_cx, rows(x_wk)).then_inc(setup_loaded[2], 16)
            sp.wait_ge(setup_drained, MIXED)
            sp.dma_start(keys, aux_keys.rearrange("(c p) d -> p c d", p=P)).then_inc(setup_loaded[3], 16)
            sp.dma_start(qw, q_proj_w).then_inc(setup_loaded[3], 16)
            sp.dma_start(uw1, unc_w1).then_inc(setup_loaded[3], 16)
            sp.dma_start(rw, router_w).then_inc(setup_loaded[3], 16)
            sp.wait_ge(setup_drained, ROUTER)
            sp.dma_start(rk32[RD:RD + 1, :], mask.rearrange("(a n) -> a n", a=1)).then_inc(mask_loaded, 16)
            sp.wait_ge(setup_drained, READY)
            sp.dma_start(cxv, row(ctx, 0).rearrange("(p j) d -> p j d", j=KC)).then_inc(ctx_loaded, 16)

            def next_ctx(b, part):
                if part == 0 or (isinstance(b, int) and b == B - 1):
                    return
                wait_full(sp, "X", FILL["X", "mix", 1], b)
                sp.dma_start(cxv, row(ctx, b + 1).rearrange("(p j) d -> p j d", j=KC)).then_inc(ctx_loaded, 16)

            def next_x(b, _):
                if isinstance(b, int) and b == B - 1:
                    return
                wait_drained(sp, "A", FILL["A", "out", 0] + 1, b)
                sp.dma_start(xa[:, :, :], tiles(row(x, b + 1))).then_inc(x_loaded, 16)

            def store_base(b, _):
                sp.wait_ge(base_ready, b + 1)
                sp.dma_start(tiles(row(base_dram, b)), x2[:, :, :]).then_inc(base_stored, 16)

            def store_agg(b, c):
                if c % PARTS == PARTS - 1:
                    t = c // PARTS
                    sp.wait_ge(summed, CHUNKS * b + c + 1)
                    sp.dma_start(tiles(row(agg_dram, b))[:, t, :], agg[:, :]).then_inc(agg_stored, 16)

            pipeline(sp, {("X", "mix"): next_ctx, ("A", "out"): next_x, ("F", "norm"): store_base,
                          ("G", "sum"): store_agg})

            sp.wait_ge(base_stored, 16 * B)
            sp.wait_ge(agg_stored, 16 * T * B)

            def reload(q):
                for k, (base_t, agg_t) in enumerate(ring):
                    wait(sp, tail_stored[k], 16 * q)
                    sp.dma_start(base_t, tiles(row(base_dram, RING * q + k))).then_inc(tail_loaded[k], 16)
                    sp.dma_start(agg_t, tiles(row(agg_dram, RING * q + k))).then_inc(tail_loaded[k], 16)

            reload(0)
            with sp.Fori(1, B // RING) as q:
                reload(q)

        @block.gpsimd
        def _(pool):
            nc.gpsimd.memset(ident[:, :], 0.0).then_inc(const_step, 1)
            pool.wait_ge(const_step, 1)
            nc.gpsimd.affine_select(out=ident[:, :], in_=ident[:, :], compare_op=ALU.not_equal, fill=1.0,
                                    base=0, pattern=[[-1, P]], channel_multiplier=1).then_inc(const_ready, 1)
            nc.gpsimd.memset(one[:, :], 1.0)
            nc.gpsimd.memset(routeT[:, :, :], 0.0)
            nc.gpsimd.memset(rwT, 0.0)
            nc.gpsimd.memset(rqS[:, :].bitcast(F32), 1.0)
            for part in qm:
                last = nc.gpsimd.memset(part[:, :, :, :].bitcast(F32), 0.0)
            last.then_inc(const_ready, 1)

            def bias_x(b, _):
                pool.wait_ge(xa_normed, b + 1)
                nc.gpsimd.tensor_tensor(xa[:, :, :], xa[:, :, :], bff[:, :].unsqueeze(1).to_broadcast([R, T, D]),
                                        ALU.add).then_inc(xa_biased, 1)

            def bias_x1(b, _):
                pool.wait_ge(x1_normed, b + 1)
                nc.gpsimd.tensor_tensor(x1[:, :, :], x1[:, :, :], cb[:, :].unsqueeze(1).to_broadcast([R, T, D]),
                                        ALU.add).then_inc(x1_biased, 1)

            def add_base(b, _):
                pool.wait_ge(x2_normed, b + 1)
                nc.gpsimd.tensor_tensor(x2[:, :, :], x2[:, :, :], xnf[:, :, :], ALU.add).then_inc(base_ready, 1)

            def gather(b, c):
                t, part = divmod(c, PARTS)
                pool.wait_ge(sc_searched, T * b + t + 1)
                wait(pool, summed, CHUNKS * b + c)
                apart(pool)
                for k in range(KG):
                    n = KG * part + k
                    pool.indirect_dma_start(vgv[:, k, :], None, aux_values,
                                            bass.IndirectOffsetOnAxis(ap=idx[:, t, n:n + 1], axis=0)).then_inc(gathered, 16)

            def next_gather(b, c):
                if c + 1 < CHUNKS:
                    gather(b, c + 1)

            def first_gather(b, t):
                if t == 1:
                    gather(b, 0)

            pool.wait_ge(small_loaded, 16 * SMALL)
            pool.wait_ge(setup_drained, FILLED)
            pipeline(pool, {("A", "norm"): bias_x, ("X", "norm"): bias_x1, ("F", "norm"): add_base,
                            ("G", "sum"): next_gather, ("F", "top"): first_gather})

        @block.scalar
        def _(act):
            def copy_out(s, j, b, dst, src):
                wait_full(act, s, j, b)
                nc.scalar.copy(dst, src).then_inc(drained[s][j % banks[s]], 1)

            def chunks(s, j):
                return bank(s, j)[:, 0:2 * S].rearrange("p (c s) -> p c s", c=2)

            def turn(s, name, dst):
                def step(b, _):
                    for j in range(2):
                        job = FILL[s, name, 0] + j
                        copy_out(s, job, b, dst[:, 2 * j:2 * j + 2, :], chunks(s, job))
                return step

            def turn_hi(b, _):
                for c in range(C):
                    job = FILL["A", "turn", 0] + c
                    wait_full(act, "A", job, b)
                    nc.scalar.copy(xT[0][:, c, :], bank("A", job)[:, 0:S]).then_inc(xT_hi, 1)

            def qk(b, k):
                j = FILL["A", "qk", k]
                wait_full(act, "A", j, b)
                for h in range(HB):
                    own = slice(h * DH, (h + 1) * DH)
                    nc.scalar.copy(qm[0][own, k % 2, h, :], bank("A", j)[own, 0:S])
                nc.scalar.copy(kT[0][:, k % 2, :], bank("A", j)[:, S:2 * S]).then_inc(qk_hi, 1)

            def value(b, _):
                for t in range(T):
                    j = FILL["A", "value", 0] + t
                    copy_out("A", j, b, va[:, t, :, :], bank("A", j)[0:R, :].rearrange("p (h d) -> p h d", h=H))

            def exp_scores(b, u):
                if u >= 1:
                    wait_full(act, "A", FILL["A", "prob", u - 1] + 1, b)
                for j in range(2):
                    job = FILL["A", "score", u] + j
                    act.wait_ge(a_maxed, 2 * UNITS * b + 2 * u + j + 1)
                    for h in (2 * j, 2 * j + 1):
                        last = nc.scalar.activation(pa[:, h, :], bank("A", job)[0:R, (h % 2) * S:(h % 2 + 1) * S],
                                                    ACT.Exp, bias=nmax[:, u % 2, h:h + 1], accum_out=rsum[:, u, h:h + 1])
                    last.then_inc(drained["A"][job % banks["A"]], 1)

            def probs_turned(b, u):
                for t in range(T):
                    j = FILL["A", "prob", u] + t
                    copy_out("A", j, b, paT[:, u % 2, t, :, :], bank("A", j)[0:R, 0:HB * R].rearrange("p (h q) -> p h q", h=HB))

            def mixed(b, u):
                k, t = divmod(u, T)
                j = FILL["A", "mix", u]
                copy_out("A", j, b, oT[:, k, t * R:(t + 1) * R], bank("A", j)[:, 0:R])

            def ctx_turned(b, part):
                for q in range(4):
                    j = FILL["X", "ctx", part] + q
                    copy_out("X", j, b, cxT[:, 2 * part + q // 2, (q % 2) * HK:(q % 2 + 1) * HK], bank("X", j)[:, 0:HK])

            def query(b, _):
                for j in range(2):
                    job = FILL["X", "query", 0] + j
                    wait_full(act, "X", job, b)
                    for k in range(2):
                        c = 2 * j + k
                        last = nc.scalar.activation(gT[:, c, :], bank("X", job)[:, k * S:(k + 1) * S],
                                                    ACT.Identity, bias=gb[:, c:c + 1])
                    last.then_inc(drained["X"][job % banks["X"]], 1)

            def x_exp(b, t):
                if t == 0:
                    wait(act, base_ready, b)
                act.wait_ge(x_maxed, T * b + t + 1)
                for j in range(2):
                    job = FILL["X", "score", t] + j
                    nc.scalar.activation(px[:, t, j * HK:(j + 1) * HK], bank("X", job)[0:R, 0:HK], ACT.Exp,
                                         bias=xmax[:, t:t + 1], accum_out=xsum[:, t, j:j + 1])\
                        .then_inc(drained["X"][job % banks["X"]], 1)

            def x_probs_turned(b, t):
                j = FILL["X", "prob", t]
                copy_out("X", j, b, pxT[:, 0:3, t * R:(t + 1) * R],
                         bank("X", j)[0:KP, 0:3 * R].rearrange("p (j q) -> p j q", j=3))

            def x_mixed(b, part):
                j = FILL["X", "mix", part]
                copy_out("X", j, b, uT[:, 2 * part:2 * part + 2, :], chunks("X", j))

            def route(b, _):
                j = FILL["F", "route", 0]
                wait(act, sc_searched, T * b)
                wait_full(act, "F", j, b)
                nc.scalar.copy(rqS[0:RD, :], bank("F", j)[0:RD, 0:S])
                nc.scalar.copy(rqS[LO:RS, :], bank("F", j)[LO:RS, 0:S])
                nc.scalar.activation(h1, bank("F", j)[:, S:2 * S], ACT.Gelu, bias=b1c[:, 0:1]).then_inc(rq_hi, 1)

            def f_score(b, t):
                wait(act, sc_searched, T * b + t)
                for n in range(4):
                    j = FILL["F", "score", t] + n
                    copy_out("F", j, b, sc[0:R, n * BANK:(n + 1) * BANK], bank("F", j)[0:R, :])

            def f_top(b, t):
                act.wait_ge(top_ready, T * b + t + 1)
                wait(act, summed, CHUNKS * (b - 1) + PARTS * (t + 1))
                nc.scalar.activation(wt[:, t, :], top[:, t, :], ACT.Exp, bias=ntop[:, t:t + 1],
                                     accum_out=wsum[:, t:t + 1]).then_inc(top_exped, 1)

            act.wait_ge(small_loaded, 16 * SMALL)
            act.wait_ge(setup_drained, READY)
            act.wait_ge(const_ready, 2)
            pipeline(act, {("A", "turn"): turn_hi, ("A", "mix"): mixed,
                           ("A", "qk"): qk, ("A", "value"): value, ("A", "score"): exp_scores, ("A", "prob"): probs_turned,
                           ("X", "ctx"): ctx_turned, ("X", "turn"): turn("X", "turn", xnxT), ("X", "query"): query,
                           ("X", "score"): x_exp, ("X", "prob"): x_probs_turned, ("X", "mix"): x_mixed,
                           ("F", "turn"): turn("F", "turn", xnfT), ("F", "route"): route, ("F", "score"): f_score,
                           ("F", "top"): f_top})

            act.wait_ge(steps["F"], F_STEPS * B)
            nc.scalar.activation(var_all[:, :], var_all[:, :], ACT.Ln, bias=1.0, accum_out=lsum[:, :])\
                .then_inc(log_done, 1)
            wait_drained(act, "F", FILL["F", "learn", 0], B - 1)
            nc.scalar.activation(gate[:, :], gate[:, :], ACT.Sigmoid, bias=b2c[:, 0:1]).then_inc(logit_done, 1)
            act.wait_ge(tail_step, 4)
            nc.scalar.activation(gate[:, :], gate[:, :], ACT.Sigmoid, scale=gwc[:, 0:1], bias=gbc[:, 0:1])\
                .then_inc(gate_ready, 1)
            with act.Fori(0, B // RING) as q:
                for k, (base_t, _) in enumerate(ring):
                    act.wait_ge(tail_added[k], q + 1)
                    act.dma_start(tiles(row(out, RING * q + k)), base_t).then_inc(tail_stored[k], 16)
            for k in range(RING):
                act.wait_ge(tail_stored[k], 16 * (B // RING))

        @block.vector
        def _(dve):
            count = {}

            def mark(s, ins):
                ins.then_inc(steps[s], 1)
                count[s] += 1

            def settle(s, b):
                dve.wait_ge(steps[s], per_batch[s] * b + count[s])

            per_batch = {"A": A_STEPS, "X": X_STEPS, "F": F_STEPS, "G": G_STEPS}

            def norm(s, b, src, dst, normed):
                count[s] = 0
                for t in range(T):
                    last = nc.vector.bn_stats(stats[s][:, t, :], src[:, t, :])
                mark(s, last)
                settle(s, b)
                apart(dve)
                for t in range(T):
                    last = nc.vector.bn_aggr(mv[s][:, t, :], stats[s][:, t, :])
                mark(s, last)
                settle(s, b)
                mark(s, nc.vector.tensor_scalar(ve[s][:, :], mv[s][:, :, 1], EPS, None, ALU.add))
                settle(s, b)
                mark(s, nc.vector.tensor_scalar(rstd[s][:, :].bitcast(I32), ve[s][:, :].bitcast(I32), -0.5, RSQRT_SEED,
                                                ALU.mult, ALU.add))
                for _ in range(3):
                    settle(s, b)
                    mark(s, nc.vector.scalar_tensor_tensor(tmp[s][:, :], rstd[s][:, :], -0.5, ve[s][:, :], ALU.mult, ALU.mult))
                    settle(s, b)
                    mark(s, nc.vector.tensor_tensor(tmp[s][:, :], tmp[s][:, :], rstd[s][:, :], ALU.mult))
                    settle(s, b)
                    mark(s, nc.vector.scalar_tensor_tensor(rstd[s][:, :], tmp[s][:, :], 1.5, rstd[s][:, :], ALU.add, ALU.mult))
                settle(s, b)
                for t in range(T):
                    last = nc.vector.tensor_scalar(dst[:, t, :], src[:, t, :], mv[s][:, t, 0:1], rstd[s][:, t:t + 1],
                                                   ALU.subtract, ALU.mult)
                last.then_inc(normed, 1)

            def a_norm(b, _):
                dve.wait_ge(x_loaded, 16 * (b + 1))
                wait_full(dve, "A", FILL["A", "turn", 0] + 3, b - 1)
                norm("A", b, xa, xo, xa_normed)

            def x_norm(b, _):
                for t in range(T):
                    wait_drained(dve, "A", FILL["A", "out", 0] + t, b)
                wait_full(dve, "X", FILL["X", "prob", 1] + 1, b - 1)
                norm("X", b, x1, xnx, x1_normed)

            def f_norm(b, _):
                for t in range(T):
                    wait_drained(dve, "X", FILL["X", "out", t], b)
                if isinstance(b, int) and b == B - 1:
                    wait_full(dve, "X", FILL["X", "prob", 1] + 1, b)
                else:
                    wait_full(dve, "X", FILL["X", "turn", 0] + 1, b + 1)
                wait(dve, base_ready, b)
                norm("F", b, x2, xnf, x2_normed)
                dve.wait_ge(x2_normed, b + 1)
                for t in range(T):
                    last = nc.vector.bn_stats(stats["F"][:, t, :], xnf[:, t, :])
                mark("F", last)
                settle("F", b)
                apart(dve)
                for t in range(T):
                    last = nc.vector.bn_aggr(mv["F"][:, t, :], stats["F"][:, t, :])
                mark("F", last)
                settle("F", b)
                mark("F", nc.vector.tensor_copy(columns(var_all, b), mv["F"][:, :, 1]))

            def lo(dst, src, hi):
                return nc.vector.tensor_tensor(dst, src, hi.bitcast(F32), ALU.subtract)

            def turn_lo(b, _):
                for c in range(C):
                    job = FILL["A", "turn", 0] + c
                    dve.wait_ge(xT_hi, C * b + c + 1)
                    lo(xT[1][:, c, :], bank("A", job)[:, 0:S], xT[0][:, c, :]).then_inc(drained["A"][job % banks["A"]], 1)

            def qk(b, k):
                j = FILL["A", "qk", k]
                dve.wait_ge(qk_hi, NB * b + k + 1)
                for h in range(HB):
                    own = slice(h * DH, (h + 1) * DH)
                    lo(qm[1][own, k % 2, h, :], bank("A", j)[own, 0:S], qm[0][own, k % 2, h, :])
                lo(kT[1][:, k % 2, :], bank("A", j)[:, S:2 * S], kT[0][:, k % 2, :]).then_inc(drained["A"][j % banks["A"]], 1)

            def maxima(b, u):
                for j in range(2):
                    job = FILL["A", "score", u] + j
                    wait_full(dve, "A", job, b)
                    nc.vector.tensor_reduce(nmax[:, u % 2, 2 * j:2 * j + 2],
                                            bank("A", job)[0:R, 0:2 * S].rearrange("p (h s) -> p h s", h=2),
                                            AX_X, ALU.max, negate=True).then_inc(a_maxed, 1)

            def share(b, u):
                for j in range(2):
                    wait_drained(dve, "A", FILL["A", "score", u] + j, b)
                mark("A", nc.vector.reciprocal(rsum[:, u, :], rsum[:, u, :]))
                settle("A", b)
                nc.vector.tensor_tensor(pa[:, :, :], pa[:, :, :], rsum[:, u, :].unsqueeze(2).to_broadcast([R, HB, S]),
                                        ALU.mult).then_inc(a_shared, 1)

            def a_out(b, _):
                assert count["A"] == A_STEPS
                dve.wait_ge(xa_biased, b + 1)
                for t in range(T):
                    wait_drained(dve, "X", FILL["X", "out", t], b - 1)
                for t in range(T):
                    j = FILL["A", "out", 0] + t
                    wait_full(dve, "A", j, b)
                    nc.vector.tensor_tensor(x1[:, t, :], bank("A", j)[0:R, :], xa[:, t, :], ALU.add)\
                        .then_inc(drained["A"][j % banks["A"]], 1)

            def x_maxima(b, t):
                for j in range(2):
                    wait_full(dve, "X", FILL["X", "score", t] + j, b)
                nc.vector.tensor_reduce(xmax[:, t:t + 1], psX[0:R, :, 0:HK], AX_XY, ALU.max, negate=True).then_inc(x_maxed, 1)

            def x_probs_turned(b, t):
                j = FILL["X", "prob", t] + 1
                wait_full(dve, "X", j, b)
                nc.vector.tensor_copy(pxT[:, 3:6, t * R:(t + 1) * R], bank("X", j)[0:KP, 0:3 * R].rearrange("p (j q) -> p j q", j=3))\
                    .then_inc(drained["X"][j % banks["X"]], 1)

            def x_out(b, t):
                if t == 0:
                    mark("X", nc.vector.tensor_tensor(xrec[:, :], xsum[:, :, 0], xsum[:, :, 1], ALU.add))
                    settle("X", b)
                    mark("X", nc.vector.reciprocal(xrec[:, :], xrec[:, :]))
                    settle("X", b)
                    assert count["X"] == X_STEPS
                    dve.wait_ge(x1_biased, b + 1)
                    wait(dve, base_stored, 16 * b)
                j = FILL["X", "out", t]
                wait_full(dve, "X", j, b)
                nc.vector.scalar_tensor_tensor(x2[:, t, :], bank("X", j)[0:R, :], xrec[:, t:t + 1], x1[:, t, :],
                                               ALU.mult, ALU.add).then_inc(drained["X"][j % banks["X"]], 1)

            def route(b, _):
                j = FILL["F", "route", 0]
                dve.wait_ge(rq_hi, b + 1)
                lo(rqS[LO:RS, :], bank("F", j)[LO:RS, 0:S], rqS[LO:RS, :]).then_inc(drained["F"][j % banks["F"]], 1)

            def learn(b, _):
                j = FILL["F", "learn", 0]
                wait_full(dve, "F", j, b)
                nc.vector.tensor_copy(columns(gate, b), bank("F", j)[0:R, 0:T]).then_inc(drained["F"][j % banks["F"]], 1)

            def f_top(b, t):
                for n in range(4):
                    wait_drained(dve, "F", FILL["F", "score", t] + n, b)
                apart(dve)
                mark("F", nc.vector.max(top[:, t, :], sc[0:R, :]))
                settle("F", b)
                nc.vector.tensor_scalar(ntop[:, t:t + 1], top[:, t, 0:1], -1.0, None, ALU.mult).then_inc(top_ready, 1)
                nc.vector.max_index(idx[:, t, :], top[:, t, :], sc[0:R, :]).then_inc(sc_searched, 1)
                assert t == 0 or count["F"] == F_STEPS

            def g_sum(b, c):
                t, part = divmod(c, PARTS)
                if c == 0:
                    count["G"] = 0
                if part == 0:
                    dve.wait_ge(top_exped, T * b + t + 1)
                    mark("G", nc.vector.reciprocal(wsum[:, t:t + 1], wsum[:, t:t + 1]))
                    settle("G", b)
                    mark("G", nc.vector.tensor_scalar(wt[:, t, :], wt[:, t, :], wsum[:, t:t + 1], None, ALU.mult))
                    settle("G", b)
                    wait(dve, agg_stored, 16 * (T * b + t))
                else:
                    dve.wait_ge(summed, CHUNKS * b + c)
                dve.wait_ge(gathered, 16 * KG * (CHUNKS * b + c + 1))
                for k in range(KG):
                    w = wt[:, t, KG * part + k:KG * part + k + 1]
                    if part == 0 and k == 0:
                        last = nc.vector.tensor_scalar(agg[:, :], vgv[:, k, :], w, None, ALU.mult)
                    else:
                        last = nc.vector.scalar_tensor_tensor(agg[:, :], vgv[:, k, :], w, agg[:, :], ALU.mult, ALU.add)
                    if k < KG - 1:
                        mark("G", last)
                        settle("G", b)
                last.then_inc(summed, 1)
                assert c < CHUNKS - 1 or count["G"] == G_STEPS

            fills = [0]

            def made():
                dve.wait_ge(setup_full, fills[0] + 1)
                fills[0] += 1
                return psA[:, (fills[0] - 1) % banks["A"], :]

            def made_parts(dst, rows=slice(0, P), scale=1.0):
                src = made()[rows, :]
                nc.vector.tensor_scalar(dst[0], src, scale, None, ALU.mult).then_inc(setup_step, 1)
                parts[0] += 1
                dve.wait_ge(setup_step, parts[0])
                nc.vector.scalar_tensor_tensor(dst[1], src, scale, dst[0].bitcast(F32), ALU.mult, ALU.subtract)\
                    .then_inc(setup_drained, 1)

            parts = [0]
            dve.wait_ge(small_loaded, 16 * SMALL)
            nc.vector.tensor_copy(bv_rows, bvc[:, :].unsqueeze(2).to_broadcast([P, C, R])).then_inc(small_step, 1)
            for w, scale in ((wqT, float(D) ** -0.5), (wkT, 1.0), (wvT, 1.0)):
                for c in range(C):
                    made_parts((w[0][:, c, :], w[1][:, c, :]), scale=scale)
            for c in range(C):
                nc.vector.tensor_copy(wffT[:, c, :], made()).then_inc(setup_drained, 1)
            for c in range(C):
                nc.vector.tensor_copy(woT[:, c, :], made()).then_inc(setup_drained, 1)
            for c in range(C):
                nc.vector.tensor_copy(m2v[:, c, :], made()).then_inc(setup_drained, 1)
            nc.vector.tensor_tensor(cb[:, :], made()[0:R, :], cb[:, :], ALU.add).then_inc(setup_drained, 1)
            for c in range(C):
                nc.vector.tensor_scalar(m1v[:, c, :], made(), float(D) ** -0.5, None, ALU.mult).then_inc(setup_drained, 1)
            nc.vector.tensor_scalar(gb[:, :], made()[:, 0:C], float(D) ** -0.5, None, ALU.mult).then_inc(setup_drained, 1)
            dve.wait_ge(const_ready, 2)
            src = made()
            nc.vector.tensor_copy(rwT[:, 0:RD], src[:, 0:RD])
            nc.vector.tensor_copy(rwT[:, LO:RS], src[:, 0:RD]).then_inc(setup_drained, 1)
            src = made()[:, 0:C * RD].rearrange("p (c r) -> p c r", c=C)
            nc.vector.tensor_copy(routeT[:, :, 0:RD], src)
            nc.vector.tensor_copy(routeT[:, :, LO:RS], src).then_inc(setup_drained, 1)
            for n in range(4):
                nc.vector.tensor_copy(keysT[:, n * BANK:(n + 1) * BANK], made()).then_inc(setup_drained, 1)
            for n in range(4):
                nc.vector.tensor_scalar(rk32[:, n * BANK:(n + 1) * BANK], made()[0:RS, :], float(RD) ** -0.5, None,
                                        ALU.mult).then_inc(setup_drained, 1)
            nc.vector.tensor_copy(unc1T[:, :, :], made().rearrange("p (c f) -> p c f", c=C)).then_inc(setup_drained, 1)
            assert fills[0] == FILLED
            dve.wait_ge(mask_loaded, 16)
            nc.vector.tensor_copy(rkS[:, :], rk32).then_inc(setup_drained, 1)
            dve.wait_ge(setup_drained, FILLED + 1)
            lo(rkL[:, :], rk32[0:RD + 1, :], rkS[0:RD + 1, :]).then_inc(setup_drained, 1)

            pipeline(dve, {("A", "norm"): a_norm, ("A", "turn"): turn_lo, ("A", "qk"): qk,
                           ("A", "score"): maxima, ("A", "share"): share,
                           ("A", "out"): a_out,
                           ("X", "norm"): x_norm, ("X", "score"): x_maxima, ("X", "prob"): x_probs_turned, ("X", "out"): x_out,
                           ("F", "norm"): f_norm, ("F", "route"): route, ("F", "learn"): learn, ("F", "top"): f_top,
                           ("G", "sum"): g_sum})

            dve.wait_ge(log_done, 1)
            nc.vector.tensor_copy(lsums, lsum[:, :].to_broadcast([R, R])).then_inc(lsum_spread, 1)
            dve.wait_ge(mean_full, 1)
            nc.vector.tensor_scalar(rmean[:, :], bank("F", 0)[0:R, 0:1], 1.0 / (B * S), 1e-6, ALU.mult, ALU.add).then_inc(tail_step, 1)
            dve.wait_ge(tail_step, 1)
            nc.vector.reciprocal(rmean[:, :], rmean[:, :]).then_inc(tail_step, 1)
            dve.wait_ge(tail_step, 2)
            nc.vector.tensor_scalar(var_all[:, :], var_all[:, :], rmean[:, 0:1], 0.5, ALU.mult, ALU.mult).then_inc(tail_step, 1)
            dve.wait_ge(tail_step, 3)
            dve.wait_ge(logit_done, 1)
            nc.vector.scalar_tensor_tensor(gate[:, :], gate[:, :], 2.5, var_all[:, :], ALU.mult, ALU.add).then_inc(clip_ready, 1)
            dve.wait_ge(clip_ready, 1)
            nc.vector.tensor_scalar(gate[:, :], gate[:, :], 0.0, 5.0, ALU.max, ALU.min).then_inc(tail_step, 1)
            dve.wait_ge(gate_ready, 1)
            with dve.Fori(0, B // RING) as q:
                for k, (base_t, agg_t) in enumerate(ring):
                    dve.wait_ge(tail_loaded[k], 32 * q + 32)
                    for t in range(T):
                        col = gate[:, bass.ds(T * RING * q + T * k + t, 1)]
                        last = nc.vector.scalar_tensor_tensor(base_t[:, t, :], agg_t[:, t, :], col, base_t[:, t, :],
                                                              ALU.mult, ALU.add)
                    last.then_inc(tail_added[k], 1)

        @block.tensor
        def _(pe):
            def product(dst, pairs):
                for n, (stationary, moving) in enumerate(pairs):
                    last = nc.tensor.matmul(dst, stationary, moving, start=n == 0, stop=n == len(pairs) - 1)
                return last

            def product3(dst, pairs):
                return product(dst, [p for s, m in pairs for p in ((s[0], m[0]), (s[0], m[1]), (s[1], m[0]))])

            def turned(dst, src):
                k = src.shape[0]
                return nc.tensor.transpose(dst, src, ident[0:k, 0:k])

            def filled(s, j, last):
                last.then_inc(full[s][j % banks[s]], 1)

            def both(parts, *at):
                return tuple(part[at] for part in parts)

            def turn(s, name, src, ready):
                a_bank = C // FILLS[s, name]

                def step(b, _):
                    ready(b)
                    for j in range(FILLS[s, name]):
                        job = FILL[s, name, 0] + j
                        wait_free(pe, s, job, b)
                        for k in range(a_bank):
                            for t in range(T):
                                at, c = k * S + t * R, a_bank * j + k
                                last = turned(bank(s, job)[:, at:at + R], src[:, t, c * P:(c + 1) * P])
                        filled(s, job, last)
                return step

            def normed(what):
                return lambda b: pe.wait_ge(what, b + 1)

            def qk(b, k):
                if k == 0:
                    wait_drained(pe, "A", FILL["A", "turn", 0] + 3, b)
                j = FILL["A", "qk", k]
                wait_free(pe, "A", j, b)
                for n, w in enumerate((wqT, wkT)):
                    last = product3(bank("A", j)[:, n * S:(n + 1) * S],
                                    [(both(w, ALL, c, slice(k * P, (k + 1) * P)), both(xT, ALL, c, ALL)) for c in range(C)])
                filled("A", j, last)

            def value(b, _):
                wait_drained(pe, "A", FILL["A", "turn", 0] + 3, b)
                for t in range(T):
                    j = FILL["A", "value", 0] + t
                    wait_free(pe, "A", j, b)
                    filled("A", j, product3(bank("A", j)[0:R, :], [(both(xT, ALL, c, slice(t * R, (t + 1) * R)),
                                                                    both(wvT, ALL, c, ALL)) for c in range(C)]))

            def a_out(b, _):
                wait_drained(pe, "A", FILL["A", "mix", UNITS - 1], b)
                for t in range(T):
                    j = FILL["A", "out", 0] + t
                    wait_free(pe, "A", j, b)
                    filled("A", j, product(bank("A", j)[0:R, :],
                                           [(oT[:, c, t * R:(t + 1) * R], wffT[:, c, :]) for c in range(C)]))

            def scores(b, u):
                k, t = divmod(u, T)
                wait_drained(pe, "A", FILL["A", "qk", k], b)
                for j in range(2):
                    job = FILL["A", "score", u] + j
                    wait_free(pe, "A", job, b)
                    for h in range(2):
                        last = product3(bank("A", job)[0:R, h * S:(h + 1) * S],
                                        [(both(qm, ALL, k % 2, 2 * j + h, slice(t * R, (t + 1) * R)), both(kT, ALL, k % 2, ALL))])
                    filled("A", job, last)

            def probs(b, u):
                pe.wait_ge(a_shared, UNITS * b + u + 1)
                for t in range(T):
                    j = FILL["A", "prob", u] + t
                    wait_free(pe, "A", j, b)
                    for h in range(HB):
                        last = turned(bank("A", j)[0:R, h * R:(h + 1) * R], pa[:, h, t * R:(t + 1) * R])
                    filled("A", j, last)

            def mixed(b, u):
                k, j = u // T, FILL["A", "mix", u]
                for t in range(T):
                    wait_drained(pe, "A", FILL["A", "prob", u] + t, b)
                if u == 0:
                    wait_drained(pe, "A", FILL["A", "value", 0] + 1, b)
                wait_free(pe, "A", j, b)
                for t in range(T):
                    for h in range(HB):
                        last = nc.tensor.matmul(bank("A", j)[h * DH:(h + 1) * DH, 0:R], va[:, t, HB * k + h, :],
                                                paT[:, u % 2, t, h, :], start=t == 0, stop=t == T - 1)
                filled("A", j, last)

            def ctx_turn(b, part):
                if part == 0:
                    pe.wait_ge(ctx_loaded, 16 * (b + 1))
                for q in range(4):
                    c, half = 2 * part + q // 2, q % 2
                    j = FILL["X", "ctx", part] + q
                    wait_free(pe, "X", j, b)
                    for k in range(3):
                        last = turned(bank("X", j)[:, k * KP:(k + 1) * KP], cxv[:, 3 * half + k, c * P:(c + 1) * P])
                    filled("X", j, last)

            def query(b, _):
                wait_drained(pe, "X", FILL["X", "turn", 0] + 1, b)
                for j in range(2):
                    job = FILL["X", "query", 0] + j
                    wait_free(pe, "X", job, b)
                    for k in range(2):
                        i = 2 * j + k
                        last = product(bank("X", job)[:, k * S:(k + 1) * S],
                                       [(m1v[:, c, i * P:(i + 1) * P], xnxT[:, c, :]) for c in range(C)])
                    filled("X", job, last)

            def x_scores(b, t):
                if t == 0:
                    for j in range(2):
                        wait_drained(pe, "X", FILL["X", "query", 0] + j, b)
                for j in range(2):
                    job = FILL["X", "score", t] + j
                    wait_free(pe, "X", job, b)
                    filled("X", job, product(bank("X", job)[0:R, 0:HK],
                                             [(gT[:, c, t * R:(t + 1) * R], cxT[:, c, j * HK:(j + 1) * HK]) for c in range(C)]))

            def x_probs(b, t):
                for j in range(2):
                    wait_drained(pe, "X", FILL["X", "score", t] + j, b)
                for j in range(2):
                    job = FILL["X", "prob", t] + j
                    wait_free(pe, "X", job, b)
                    for k in range(3):
                        n = 3 * j + k
                        last = turned(bank("X", job)[0:KP, k * R:(k + 1) * R], px[:, t, n * KP:(n + 1) * KP])
                    filled("X", job, last)

            def x_mix(b, part):
                if part == 0:
                    for j in range(2):
                        wait_drained(pe, "X", FILL["X", "prob", 1] + j, b)
                job = FILL["X", "mix", part]
                wait_free(pe, "X", job, b)
                for k in range(2):
                    i = 2 * part + k
                    last = product(bank("X", job)[:, k * S:(k + 1) * S],
                                   [(cxv[:, n, i * P:(i + 1) * P], pxT[:, n, :]) for n in range(KC)])
                filled("X", job, last)

            def x_out(b, t):
                if t == 0:
                    wait_drained(pe, "X", FILL["X", "mix", 1], b)
                job = FILL["X", "out", t]
                wait_free(pe, "X", job, b)
                filled("X", job, product(bank("X", job)[0:R, :],
                                         [(uT[:, c, t * R:(t + 1) * R], m2v[:, c, :]) for c in range(C)]))

            def route(b, _):
                wait_drained(pe, "F", FILL["F", "turn", 0] + 1, b)
                j = FILL["F", "route", 0]
                wait_free(pe, "F", j, b)
                product(bank("F", j)[0:RS, 0:S], [(routeT[:, c, :], xnfT[:, c, :]) for c in range(C)])
                filled("F", j, product(bank("F", j)[:, S:2 * S], [(unc1T[:, c, :], xnfT[:, c, :]) for c in range(C)]))

            def learn(b, _):
                wait_drained(pe, "F", FILL["F", "route", 0], b)
                j = FILL["F", "learn", 0]
                wait_free(pe, "F", j, b)
                for t in range(T):
                    last = product(bank("F", j)[0:R, t:t + 1], [(h1[:, t * R:(t + 1) * R], w2c[:, :])])
                filled("F", j, last)

            def f_scores(b, t):
                tile = slice(t * R, (t + 1) * R)
                for n in range(4):
                    j = FILL["F", "score", t] + n
                    cols = slice(n * BANK, (n + 1) * BANK)
                    wait_free(pe, "F", j, b)
                    filled("F", j, product(bank("F", j)[0:R, :],
                                           [(rqS[:, tile], rkS[:, cols]), (rqS[0:RD + 1, tile], rkL[:, cols])]))

            fills = [0]

            def place():
                wait(pe, setup_drained, fills[0] - banks["A"] + 1)
                fills[0] += 1
                return psA[:, (fills[0] - 1) % banks["A"], :]

            def turn_weight(w):
                for i in range(C):
                    dst = place()
                    for o in range(C):
                        last = turned(dst[:, o * P:(o + 1) * P], w[:, o, i * P:(i + 1) * P])
                    last.then_inc(setup_full, 1)

            pe.wait_ge(const_ready, 1)
            pe.wait_ge(setup_loaded[0], 16 * 4)
            for w in (at_cx, at_m1, at_sc, at_big):
                turn_weight(w)
            pe.wait_ge(setup_loaded[1], 16 * 3)
            turn_weight(at_cx)
            pe.wait_ge(setup_drained, WO)
            for i in range(C):
                product(place(), [(at_m1[:, e, i * P:(i + 1) * P], woT[:, e, :]) for e in range(C)]).then_inc(setup_full, 1)
            pe.wait_ge(small_step, 1)
            product(place()[0:R, :], [(bv_rows[:, e, :], woT[:, e, :]) for e in range(C)]).then_inc(setup_full, 1)
            pe.wait_ge(setup_loaded[2], 16)
            for i in range(C):
                product(place(), [(at_sc[:, e, i * P:(i + 1) * P], at_cx[:, e, :]) for e in range(C)]).then_inc(setup_full, 1)
            dst = place()
            for i in range(C):
                last = product(dst[:, i:i + 1], [(at_cx[:, e, i * P:(i + 1) * P], bqc[:, e:e + 1]) for e in range(C)])
            last.then_inc(setup_full, 1)
            pe.wait_ge(setup_loaded[3], 16 * 4)
            turned(place()[:, 0:RD], rw).then_inc(setup_full, 1)
            pe.wait_ge(setup_drained, fills[0])
            dst = place()
            for i in range(C):
                last = product(dst[:, i * RD:(i + 1) * RD], [(qw[:, i * P:(i + 1) * P], rwT[:, 0:RD])])
            last.then_inc(setup_full, 1)
            for n in range(4):
                dst = place()
                for k in range(4):
                    last = turned(dst[:, k * P:(k + 1) * P], keys[:, 4 * n + k, :])
                last.then_inc(setup_full, 1)
            pe.wait_ge(setup_drained, fills[0])
            for n in range(4):
                product(place()[0:RS, :], [(rwT, keysT[:, n * BANK:(n + 1) * BANK])]).then_inc(setup_full, 1)
            dst = place()
            for i in range(C):
                last = turned(dst[:, i * P:(i + 1) * P], uw1[:, i * P:(i + 1) * P])
            last.then_inc(setup_full, 1)
            pe.wait_ge(setup_drained, READY)

            pipeline(pe, {("A", "turn"): turn("A", "turn", xo, normed(xa_normed)),
                          ("X", "turn"): turn("X", "turn", xnx, normed(x1_normed)),
                          ("F", "turn"): turn("F", "turn", xnf, normed(x2_normed)),
                          ("A", "qk"): qk, ("A", "value"): value, ("A", "score"): scores,
                          ("A", "prob"): probs, ("A", "mix"): mixed, ("A", "out"): a_out,
                          ("X", "ctx"): ctx_turn, ("X", "query"): query, ("X", "score"): x_scores,
                          ("X", "prob"): x_probs, ("X", "mix"): x_mix, ("X", "out"): x_out,
                          ("F", "route"): route, ("F", "learn"): learn, ("F", "score"): f_scores})

            pe.wait_ge(lsum_spread, 1)
            wait_free(pe, "F", 0, B)
            product(bank("F", 0)[0:R, 0:1], [(lsums, one[:, :])]).then_inc(mean_full, 1)


_INS = ['x', 'ctx_1024', 'L0_attn_Wq', 'L0_attn_Wk', 'L0_attn_Wv', 'L0_attn_Wff', 'L0_attn_bff', 'L0_xattn_Wk',
        'L0_xattn_Wv', 'L0_xattn_bv', 'L0_xattn_Wq', 'L0_xattn_bq', 'L0_xattn_Wo', 'L0_xattn_bo',
        'L0_ffn_q_proj_w', 'L0_ffn_router_w', 'L0_ffn_aux_keys', 'L0_ffn_aux_values', 'L0_ffn_reliability_mask',
        'L0_ffn_unc_w1', 'L0_ffn_unc_b1', 'L0_ffn_unc_w2', 'L0_ffn_unc_b2', 'L0_ffn_gate_w1', 'L0_ffn_gate_bias']


def kernel(**inputs):
    import numpy as np
    import concourse.bacc as bacc
    from concourse.bass_utils import run_bass_kernel_spmd

    nc = bacc.Bacc("TRN2", target_bir_lowering=False, num_devices=1)
    arrays, args = {}, []
    for name in _INS:
        a = np.ascontiguousarray(inputs[name])
        if a.ndim == 0:
            a = a.reshape(1)
        arrays[f"in_{name}"] = a
        args.append(nc.dram_tensor(f"in_{name}", a.shape, mybir.dt.from_np(a.dtype), kind="ExternalInput").ap())
    out = nc.dram_tensor("out", [B, S, D], F32, kind="ExternalOutput").ap()
    build(nc, *args, out)
    return run_bass_kernel_spmd(nc, [arrays], core_ids=[0]).results[0]["out"]
```

```python
from contextlib import ExitStack

import concourse.bass as bass
from concourse import mybir

F32 = mybir.dt.float32
F32R = mybir.dt.float32r
I32 = mybir.dt.int32
U32 = mybir.dt.uint32
ALL = slice(None)
ALU = mybir.AluOpType
ACT = mybir.ActivationFunctionType
AX_X = mybir.AxisListType.X
AX_XY = mybir.AxisListType.XY

P = 128
B, S, D = 32, 224, 512
C = D // P
T, R = 2, S // 2
H = 16
DH = D // H
HB = P // DH
NB = H // HB
UNITS = NB * T
SK = 750
KC = 6
KP = SK // KC
HK = SK // 2
N, K8, RD = 2048, 8, 48
BOT = 128
LO = 64
RS = LO + RD
KG = 2
PARTS = K8 // KG
CHUNKS = T * PARTS
BANK = 512
EPS = 1e-5
RSQRT_SEED = 1597463007.0

BANKS = {"A": 4, "X": 2, "F": 2}

ORDER = (
    ("A", "norm", 0), ("X", "enter", 0), ("A", "turn", 0), ("X", "ctx", 0), ("X", "norm", 0), ("X", "ctx", 1),
    ("A", "value", 0), ("G", "sum", 0), ("X", "turn", 0), ("F", "norm", 0), ("A", "qk", 0), ("G", "sum", 1),
    ("X", "ctx", 2), ("A", "qk", 1), ("X", "query", 0), ("F", "turn", 0), ("X", "ctx", 3), ("G", "sum", 2),
    ("A", "score", 0), ("X", "score", 0), ("G", "sum", 3), ("A", "share", 0), ("F", "route", 0), ("X", "score", 1),
    ("A", "prob", 0), ("A", "score", 1), ("F", "learn", 0), ("X", "prob", 0), ("A", "share", 1), ("A", "qk", 2),
    ("X", "prob", 1), ("F", "score", 0), ("A", "prob", 1), ("A", "score", 2), ("A", "mix", 0), ("A", "share", 2),
    ("A", "mix", 1), ("A", "score", 3), ("G", "sum", 4), ("F", "score", 1), ("A", "prob", 2), ("X", "mix", 0),
    ("A", "mix", 2), ("A", "share", 3), ("A", "prob", 3), ("F", "top", 0), ("A", "score", 4), ("A", "share", 4),
    ("A", "qk", 3), ("X", "mix", 1), ("G", "sum", 5), ("A", "mix", 3), ("A", "prob", 4), ("A", "score", 5),
    ("F", "score", 2), ("A", "share", 5), ("A", "mix", 4), ("A", "score", 6), ("F", "score", 3), ("G", "sum", 6),
    ("A", "share", 6), ("A", "prob", 5), ("X", "out", 0), ("A", "score", 7), ("G", "sum", 7), ("A", "share", 7),
    ("A", "prob", 6), ("X", "out", 1), ("A", "mix", 5), ("A", "prob", 7), ("A", "mix", 6), ("A", "mix", 7),
    ("F", "top", 1),
)

FILLS = {("A", "turn"): 2, ("A", "qk"): 1, ("A", "value"): 2, ("A", "score"): 2, ("A", "prob"): 2,
         ("A", "mix"): 1,
         ("X", "enter"): 2, ("X", "ctx"): 2, ("X", "turn"): 2, ("X", "query"): 2, ("X", "score"): 2, ("X", "prob"): 2,
         ("X", "mix"): 1, ("X", "out"): 1,
         ("F", "turn"): 2, ("F", "route"): 1, ("F", "learn"): 1, ("F", "score"): 2}
FILL = {}
JOBS = {"A": 0, "X": 0, "F": 0}
for _s, _step, _arg in ORDER:
    if (_s, _step) in FILLS:
        FILL[_s, _step, _arg] = JOBS[_s]
        JOBS[_s] += FILLS[_s, _step]
assert all(JOBS[_s] % BANKS[_s] == 0 for _s in JOBS)

A_STEPS, X_STEPS, F_STEPS, G_STEPS = 21, 15, 18, 12


def build(nc, x, ctx, attn_wq, attn_wk, attn_wv, attn_wff, attn_bff, x_wk, x_wv, x_bv, x_wq, x_bq,
          x_wo, x_bo, q_proj_w, router_w, aux_keys, aux_values, mask, unc_w1, unc_b1, unc_w2,
          unc_b2, gate_w1, gate_bias, out):
    stack = ExitStack()
    with stack:
        def sb(name, shape, dt=F32):
            return stack.enter_context(nc.sbuf_tensor(name, shape, dt))

        def sem(name):
            return stack.enter_context(nc.semaphore(name))

        base_dram = nc.dram_tensor("base_scratch", [B, S, D], F32).ap()
        agg_dram = nc.dram_tensor("agg_scratch", [B, S, D], F32).ap()

        wqT, wkT, wvT = ((sb(n + "_hi", [P, C, D], F32R), sb(n + "_lo", [P, C, D], F32R)) for n in ("wqT", "wkT", "wvT"))
        wffT = sb("wffT", [P, C, D])
        m1, m2 = sb("m1", [P, C * D]), sb("m2", [P, C * D])
        rkS = sb("rkS", [RS, N], F32R)
        rkL = sb("rkL", [RD + 1, N], F32R)
        routeT = sb("routeT", [P, C, RS])
        unc1T = sb("unc1T", [P, C, BOT])
        ident = sb("ident", [P, P])
        bff = sb("bff", [R, D])
        cb = sb("cb", [R, D])
        bvc, bqc, gb = (sb(n, [P, C]) for n in ("bvc", "bqc", "gb"))
        b1c, w2c = sb("b1c", [P, 1]), sb("w2c", [P, 1])
        b2c, gwc, gbc = (sb(n, [R, 1]) for n in ("b2c", "gwc", "gbc"))

        xa = sb("xa", [R, T, D])
        xT = (sb("xT_hi", [P, C, S], F32R), sb("xT_lo", [P, C, S], F32R))
        qm = (sb("qm_hi", [P, 2, HB, S], F32R), sb("qm_lo", [P, 2, HB, S], F32R))
        kT = (sb("kT_hi", [P, 2, S], F32R), sb("kT_lo", [P, 2, S], F32R))
        va = sb("va", [R, T, H, DH])
        nmax = sb("nmax", [R, 2, HB])
        rsum = sb("rsum", [R, UNITS, HB])
        pa = sb("pa", [R, HB, S])
        oT = sb("oT", [P, C, S])
        big = sb("big", [P, C * SK])
        paT = big[0:R, 0:2 * HB * S].rearrange("p (a t h q) -> p a t h q", a=2, t=T, h=HB)
        cxT = big[:, :].rearrange("p (c k) -> p c k", c=C)
        xr = sb("xr", [R, T, D])
        x1 = sb("x1", [R, T, D])
        nx = sb("nx", [R, T * SK])
        xnx = nx[:, 0:T * D].rearrange("p (t d) -> p t d", t=T)
        xnf = xnx
        px = nx[:, :].rearrange("p (t k) -> p t k", t=T)
        xnxT = sb("xnxT", [P, C, S])
        uT = xnxT
        gT = sb("gT", [P, C, S])
        cx = sb("cx", [P, KC * D])
        cxv = cx[0:KP, :].rearrange("p (j d) -> p j d", j=KC)
        pT = sb("pT", [P, KC, S])
        pxT = pT[0:KP, :, :]
        xnfT = pT[:, 0:C, :]
        xmax = sb("xmax", [R, T])
        xsum = sb("xsum", [R, T, 2])
        xrec = sb("xrec", [R, T])
        x2 = sb("x2", [R, T, D])
        rqS = sb("rqS", [RS, S], F32R)
        sc = sb("sc", [P, N])
        h1 = sc[0:BOT, 0:S]
        top = sb("top", [R, T, K8])
        ntop = sb("ntop", [R, T])
        idx = sb("idx", [R, T, K8], U32)
        wt = sb("wt", [R, T, K8])
        wsum = sb("wsum", [R, T])
        vg = sb("vg", [P, KG * D])
        vgv = vg[0:R, :].rearrange("p (k d) -> p k d", k=KG)
        agg = sb("agg", [R, D])
        stats = {s: sb(f"stats_{s}", [R, T, 6]) for s in "AXF"}
        mv = {s: sb(f"mv_{s}", [R, T, 2]) for s in "AXF"}
        ve = {s: sb(f"ve_{s}", [R, T]) for s in "AXF"}
        rstd = {s: sb(f"rstd_{s}", [R, T]) for s in "AXF"}
        tmp = {s: sb(f"tmp_{s}", [R, T]) for s in "AXF"}
        var_all = sb("var_all", [R, B * T])
        gate = sb("gate", [R, B * T])
        lsum, one = sb("lsum", [R, 1]), sb("one", [R, 1])
        lsums = gT[0:R, 0, 0:R]
        rmean = sb("rmean", [R, 1])

        psA = stack.enter_context(nc.psum_tensor("psA", [P, BANKS["A"], BANK], F32))
        psX = stack.enter_context(nc.psum_tensor("psX", [P, BANKS["X"], BANK], F32))
        psF = stack.enter_context(nc.psum_tensor("psF", [P, BANKS["F"], BANK], F32))
        ps = {"A": psA, "X": psX, "F": psF}
        banks, jobs = BANKS, JOBS
        full = {s: [sem(f"{s}_full{k}") for k in range(n)] for s, n in banks.items()}
        drained = {s: [sem(f"{s}_drained{k}") for k in range(n)] for s, n in banks.items()}

        weight_loaded = [sem(f"weight_loaded{k}") for k in range(5)]
        cross_loaded = [sem(f"cross_loaded{k}") for k in range(3)]
        look_up_loaded = sem("look_up_loaded")
        setup_full, setup_drained = sem("setup_full"), sem("setup_drained")
        const_step, const_ready = sem("const_step"), sem("const_ready")
        small_step, setup_hi = sem("small_step"), sem("setup_hi")
        waited = sem("waited")
        x_loaded, xr_loaded, ctx_loaded = sem("x_loaded"), sem("xr_loaded"), sem("ctx_loaded")
        xa_normed, xr_biased = sem("xa_normed"), sem("xr_biased")
        x1_normed, x1_biased = sem("x1_normed"), sem("x1_biased")
        x2_normed, base_ready, base_stored = sem("x2_normed"), sem("base_ready"), sem("base_stored")
        a_maxed, a_shared, x_maxed = sem("a_maxed"), sem("a_shared"), sem("x_maxed")
        sc_searched, top_ready, top_exped = sem("sc_searched"), sem("top_ready"), sem("top_exped")
        gathered, summed, agg_stored = sem("gathered"), sem("summed"), sem("agg_stored")
        xT_hi, qk_hi, rq_hi = sem("xT_hi"), sem("qk_hi"), sem("rq_hi")
        small_loaded, mask_loaded = sem("small_loaded"), sem("mask_loaded")
        steps = {s: sem(f"dve_step_{s}") for s in "AXFG"}
        log_done, lsum_spread, mean_full = sem("log_done"), sem("lsum_spread"), sem("mean_full")
        tail_step, gate_ready = sem("tail_step"), sem("gate_ready")
        logit_done, clip_ready = sem("logit_done"), sem("clip_ready")

        def wait(eng, s, value):
            if not (isinstance(value, int) and value <= 0):
                eng.wait_ge(s, value)

        def apart(eng):
            eng.sem_inc(waited, 1)

        def bank(s, j):
            return ps[s][:, j % banks[s], :]

        def nth(s, j, b):
            return jobs[s] // banks[s] * b + j // banks[s]

        def wait_free(eng, s, j, b):
            wait(eng, drained[s][j % banks[s]], nth(s, j, b))

        def wait_full(eng, s, j, b):
            wait(eng, full[s][j % banks[s]], nth(s, j, b) + 1)

        def wait_drained(eng, s, j, b):
            wait(eng, drained[s][j % banks[s]], nth(s, j, b) + 1)

        def pipeline(eng, step):
            def iteration(i):
                batch = {"A": i, "X": i - 1, "F": i - 2, "G": i - 3}
                for s, name, arg in ORDER:
                    b = batch[s]
                    outside = isinstance(b, int) and not 0 <= b < B
                    if (s, name) in step and not outside:
                        step[s, name](b, arg)

            for i in range(3):
                iteration(i)
            with eng.Fori(3, B - 1) as i:
                iteration(i)
            for i in range(B - 1, B + 2):
                iteration(i)

        def row(t, b):
            return t[b, :, :] if isinstance(b, int) else t[bass.ds(b, 1), :, :].rearrange("a s d -> (a s) d")

        def tiles(a):
            return a.rearrange("(t r) d -> r t d", r=R)

        def columns(a, b):
            return a[:, T * b:T * b + T] if isinstance(b, int) else a[:, bass.ds(T * b, T)]

        def weight(a):
            return a[:, 0:C * D].rearrange("p (c d) -> p c d", c=C)

        at_cx, at_m1, at_m2, at_sc, at_big = (weight(a) for a in (cx, m1, m2, sc, big))
        woT = at_big
        keys, keysT = big[:, 0:N].rearrange("p (c d) -> p c d", d=BOT), sc[:, :]
        qw, uw1, rw = cx[:, C * D:(C + 1) * D], cx[:, (C + 1) * D:(C + 2) * D], vg[0:RD, 0:BOT]
        rk32 = cx[0:RS, 0:N]
        rwT = gT[:, 0, 0:RS]
        bv_rows = uT[:, :, 0:R]
        m1v, m2v = weight(m1), weight(m2)
        WO, VALUED, MIXED = 16 + 4, 20 + 4 + 1, 25 + 4 + 1
        ROUTER, FILLED = MIXED + 1 + 1 + 4 + 4, MIXED + 1 + 1 + 4 + 4 + 1
        READY = FILLED + 2
        SMALL = 9

        ring = [(w[0:R, 0:T * D].rearrange("p (t d) -> p t d", t=T),
                 w[0:R, T * D:2 * T * D].rearrange("p (t d) -> p t d", t=T))
                for w in (m1, m2, cx, big, wffT[:, :, :].rearrange("p c d -> p (c d)"))]
        ring += [(xa, xr), (x1, x2), (sc[0:R, 0:T * D].rearrange("p (t d) -> p t d", t=T),
                                      sc[0:R, T * D:2 * T * D].rearrange("p (t d) -> p t d", t=T))]
        RING = len(ring)
        assert 3 * CHUNKS == B - RING
        tail_loaded = [sem(f"tail_loaded{k}") for k in range(RING)]
        tail_added = [sem(f"tail_added{k}") for k in range(RING)]
        tail_stored = [sem(f"tail_stored{k}") for k in range(RING)]

        block = stack.enter_context(nc.Block())

        @block.sync
        def _(sp):
            def rows(w):
                return w.rearrange("(c p) d -> p c d", p=P)

            def small(dst, src):
                sp.dma_start(dst, src).then_inc(small_loaded, 16)

            for n, (place, w) in enumerate(((at_cx, attn_wq), (at_m1, attn_wk), (at_sc, attn_wv), (at_big, attn_wff),
                                            (at_m2, x_wo))):
                sp.dma_start(place, rows(w)).then_inc(weight_loaded[n], 16)
            for n, (place, w) in enumerate(((at_cx, x_wk), (at_m1, x_wv), (at_sc, x_wq))):
                sp.wait_ge(setup_drained, C * (n + 1))
                sp.dma_start(place, rows(w)).then_inc(cross_loaded[n], 16)
            with nc.allow_non_contiguous_dma(reason="bias columns, once"):
                small(bvc[:, :], x_bv.rearrange("(c p) -> p c", p=P))
                small(bqc[:, :], x_bq.rearrange("(c p) -> p c", p=P))
                small(b1c[:, :], unc_b1.rearrange("(p a) -> p a", a=1))
                small(w2c[:, :], unc_w2.rearrange("a p -> p a"))
            small(bff[:, :], attn_bff.partition_broadcast(R))
            small(cb[:, :], x_bo.partition_broadcast(R))
            small(b2c[:, :], unc_b2.partition_broadcast(R))
            small(gwc[:, :], gate_w1.partition_broadcast(R))
            small(gbc[:, :], gate_bias.partition_broadcast(R))
            sp.dma_start(xa[:, :, :], tiles(row(x, 0))).then_inc(x_loaded, 16)
            sp.dma_start(xr[:, :, :], tiles(row(x, 0))).then_inc(xr_loaded, 16)
            sp.dma_start(qw, q_proj_w).then_inc(look_up_loaded, 16)
            sp.dma_start(uw1, unc_w1).then_inc(look_up_loaded, 16)
            sp.dma_start(rw, router_w).then_inc(look_up_loaded, 16)
            sp.wait_ge(setup_drained, VALUED)
            sp.dma_start(keys, aux_keys.rearrange("(c p) d -> p c d", p=P)).then_inc(look_up_loaded, 16)
            sp.wait_ge(setup_drained, ROUTER)
            sp.dma_start(rk32[RD:RD + 1, :], mask.rearrange("(a n) -> a n", a=1)).then_inc(mask_loaded, 16)
            sp.wait_ge(setup_drained, READY)
            sp.dma_start(cxv, row(ctx, 0).rearrange("(p j) d -> p j d", j=KC)).then_inc(ctx_loaded, 16)

            def next_ctx(b, part):
                if part == 0 or (isinstance(b, int) and b == B - 1):
                    return
                wait_full(sp, "X", FILL["X", "mix", 1], b)
                sp.dma_start(cxv, row(ctx, b + 1).rearrange("(p j) d -> p j d", j=KC)).then_inc(ctx_loaded, 16)

            def next_x(b, _):
                if isinstance(b, int) and b == B - 1:
                    return
                wait_full(sp, "A", FILL["A", "turn", 0] + 1, b)
                sp.dma_start(xa[:, :, :], tiles(row(x, b + 1))).then_inc(x_loaded, 16)

            def next_xr(b, _):
                if isinstance(b, int) and b == B - 1:
                    return
                wait_drained(sp, "X", FILL["X", "enter", 0] + 1, b)
                sp.dma_start(xr[:, :, :], tiles(row(x, b + 1))).then_inc(xr_loaded, 16)

            def store_base(b, _):
                sp.wait_ge(base_ready, b + 1)
                sp.dma_start(tiles(row(base_dram, b)), x2[:, :, :]).then_inc(base_stored, 16)

            def store_agg(b, c):
                if c % PARTS == PARTS - 1:
                    t = c // PARTS
                    sp.wait_ge(summed, CHUNKS * b + c + 1)
                    sp.dma_start(tiles(row(agg_dram, b))[:, t, :], agg[:, :]).then_inc(agg_stored, 16)

            pipeline(sp, {("X", "mix"): next_ctx, ("A", "turn"): next_x, ("X", "enter"): next_xr,
                          ("F", "norm"): store_base,
                          ("G", "sum"): store_agg})

            sp.wait_ge(base_stored, 16 * B)
            sp.wait_ge(agg_stored, 16 * T * (B - 1))

            for q in range(B // RING):
                for k, (base_t, agg_t) in enumerate(ring):
                    if q == 0 and k == RING - 1:
                        sp.wait_ge(sc_searched, T * B)
                    if q == B // RING - 1 and k == RING - 1:
                        sp.wait_ge(agg_stored, 16 * T * B)
                    wait(sp, tail_stored[k], 16 * q)
                    sp.dma_start(base_t[:, :, :], tiles(row(base_dram, RING * q + k))).then_inc(tail_loaded[k], 16)
                    sp.dma_start(agg_t[:, :, :], tiles(row(agg_dram, RING * q + k))).then_inc(tail_loaded[k], 16)
                    if (q, k) == (B // RING - 2, 0):
                        store_agg(B - 1, PARTS - 1)
                    if (q, k) == (B // RING - 1, RING - 2):
                        store_agg(B - 1, CHUNKS - 1)

        @block.gpsimd
        def _(pool):
            nc.gpsimd.memset(ident[:, :], 0.0).then_inc(const_step, 1)
            pool.wait_ge(const_step, 1)
            nc.gpsimd.affine_select(out=ident[:, :], in_=ident[:, :], compare_op=ALU.not_equal, fill=1.0,
                                    base=0, pattern=[[-1, P]], channel_multiplier=1).then_inc(const_ready, 1)
            nc.gpsimd.memset(one[:, :], 1.0)
            nc.gpsimd.memset(routeT[:, :, :], 0.0)
            nc.gpsimd.memset(rwT, 0.0)
            nc.gpsimd.memset(rqS[:, :].bitcast(F32), 1.0)
            for part in qm:
                last = nc.gpsimd.memset(part[:, :, :, :].bitcast(F32), 0.0)
            last.then_inc(const_ready, 1)

            def bias_x(b, u):
                if u == 0:
                    pool.wait_ge(xr_loaded, 16 * (b + 1))
                    nc.gpsimd.tensor_tensor(xr[:, :, :], xr[:, :, :], bff[:, :].unsqueeze(1).to_broadcast([R, T, D]),
                                            ALU.add).then_inc(xr_biased, 1)

            def bias_x1(b, _):
                pool.wait_ge(x1_normed, b + 1)
                nc.gpsimd.tensor_tensor(x1[:, :, :], x1[:, :, :], cb[:, :].unsqueeze(1).to_broadcast([R, T, D]),
                                        ALU.add).then_inc(x1_biased, 1)

            def add_base(b, _):
                pool.wait_ge(x2_normed, b + 1)
                nc.gpsimd.tensor_tensor(x2[:, :, :], x2[:, :, :], xnf[:, :, :], ALU.add).then_inc(base_ready, 1)

            def gather(b, c):
                t, part = divmod(c, PARTS)
                pool.wait_ge(sc_searched, T * b + t + 1)
                wait(pool, summed, CHUNKS * b + c)
                apart(pool)
                for k in range(KG):
                    n = KG * part + k
                    pool.indirect_dma_start(vgv[:, k, :], None, aux_values,
                                            bass.IndirectOffsetOnAxis(ap=idx[:, t, n:n + 1], axis=0)).then_inc(gathered, 16)

            def next_gather(b, c):
                if c + 1 < CHUNKS:
                    gather(b, c + 1)

            def first_gather(b, t):
                if t == 1:
                    gather(b, 0)

            pool.wait_ge(small_loaded, 16 * SMALL)
            pool.wait_ge(setup_drained, FILLED)
            pipeline(pool, {("A", "mix"): bias_x, ("X", "norm"): bias_x1, ("F", "norm"): add_base,
                            ("G", "sum"): next_gather, ("F", "top"): first_gather})
            for c in range(CHUNKS):
                next_gather(B - 1, c)

        @block.scalar
        def _(act):
            def copy_out(s, j, b, dst, src):
                wait_full(act, s, j, b)
                nc.scalar.copy(dst, src).then_inc(drained[s][j % banks[s]], 1)

            def chunks(s, j):
                return bank(s, j)[:, 0:2 * S].rearrange("p (c s) -> p c s", c=2)

            def turn(s, name, dst):
                def step(b, _):
                    for j in range(2):
                        job = FILL[s, name, 0] + j
                        copy_out(s, job, b, dst[:, 2 * j:2 * j + 2, :], chunks(s, job))
                return step

            def turn_hi(b, _):
                for j in range(2):
                    job = FILL["A", "turn", 0] + j
                    wait_full(act, "A", job, b)
                    nc.scalar.copy(xT[0][:, 2 * j:2 * j + 2, :], chunks("A", job)).then_inc(xT_hi, 1)

            def qk(b, k):
                j = FILL["A", "qk", k]
                wait_full(act, "A", j, b)
                for h in range(HB):
                    own = slice(h * DH, (h + 1) * DH)
                    nc.scalar.copy(qm[0][own, k % 2, h, :], bank("A", j)[own, 0:S])
                nc.scalar.copy(kT[0][:, k % 2, :], bank("A", j)[:, S:2 * S]).then_inc(qk_hi, 1)

            def value(b, _):
                for t in range(T):
                    j = FILL["A", "value", 0] + t
                    copy_out("A", j, b, va[:, t, :, :], bank("A", j)[0:R, :].rearrange("p (h d) -> p h d", h=H))

            def exp_scores(b, u):
                if u >= 1:
                    wait_full(act, "A", FILL["A", "prob", u - 1] + 1, b)
                for j in range(2):
                    job = FILL["A", "score", u] + j
                    act.wait_ge(a_maxed, 2 * UNITS * b + 2 * u + j + 1)
                    for h in (2 * j, 2 * j + 1):
                        last = nc.scalar.activation(pa[:, h, :], bank("A", job)[0:R, (h % 2) * S:(h % 2 + 1) * S],
                                                    ACT.Exp, bias=nmax[:, u % 2, h:h + 1], accum_out=rsum[:, u, h:h + 1])
                    last.then_inc(drained["A"][job % banks["A"]], 1)

            def probs_turned(b, u):
                for t in range(T):
                    j = FILL["A", "prob", u] + t
                    copy_out("A", j, b, paT[:, u % 2, t, :, :], bank("A", j)[0:R, 0:HB * R].rearrange("p (h q) -> p h q", h=HB))

            def mixed(b, u):
                k, t = divmod(u, T)
                j = FILL["A", "mix", u]
                copy_out("A", j, b, oT[:, k, t * R:(t + 1) * R], bank("A", j)[:, 0:R])

            def ctx_turned(b, c):
                for half in range(2):
                    j = FILL["X", "ctx", c] + half
                    copy_out("X", j, b, cxT[:, c, half * HK:(half + 1) * HK], bank("X", j)[:, 0:HK])

            def query(b, _):
                for j in range(2):
                    job = FILL["X", "query", 0] + j
                    wait_full(act, "X", job, b)
                    for k in range(2):
                        c = 2 * j + k
                        last = nc.scalar.activation(gT[:, c, :], bank("X", job)[:, k * S:(k + 1) * S],
                                                    ACT.Identity, bias=gb[:, c:c + 1])
                    last.then_inc(drained["X"][job % banks["X"]], 1)

            def x_exp(b, t):
                if t == 0:
                    wait(act, base_ready, b)
                act.wait_ge(x_maxed, T * b + t + 1)
                for j in range(2):
                    job = FILL["X", "score", t] + j
                    nc.scalar.activation(px[:, t, j * HK:(j + 1) * HK], bank("X", job)[0:R, 0:HK], ACT.Exp,
                                         bias=xmax[:, t:t + 1], accum_out=xsum[:, t, j:j + 1])\
                        .then_inc(drained["X"][job % banks["X"]], 1)

            def x_probs_turned(b, t):
                j = FILL["X", "prob", t]
                copy_out("X", j, b, pxT[:, 0:3, t * R:(t + 1) * R],
                         bank("X", j)[0:KP, 0:3 * R].rearrange("p (j q) -> p j q", j=3))

            def x_mixed(b, part):
                j = FILL["X", "mix", part]
                copy_out("X", j, b, uT[:, 2 * part:2 * part + 2, :], chunks("X", j))

            def route(b, _):
                j = FILL["F", "route", 0]
                wait(act, sc_searched, T * b)
                wait_full(act, "F", j, b)
                nc.scalar.copy(rqS[0:RD, :], bank("F", j)[0:RD, 0:S])
                nc.scalar.copy(rqS[LO:RS, :], bank("F", j)[LO:RS, 0:S])
                nc.scalar.activation(h1, bank("F", j)[:, S:2 * S], ACT.Gelu, bias=b1c[:, 0:1]).then_inc(rq_hi, 1)

            def f_score(b, part):
                t, half = divmod(part, 2)
                if half == 0:
                    wait(act, sc_searched, T * b + t)
                for n in (2 * half, 2 * half + 1):
                    j = FILL["F", "score", part] + n % 2
                    copy_out("F", j, b, sc[0:R, n * BANK:(n + 1) * BANK], bank("F", j)[0:R, :])

            def f_top(b, t):
                act.wait_ge(top_ready, T * b + t + 1)
                wait(act, summed, CHUNKS * (b - 1) + PARTS * (t + 1))
                nc.scalar.activation(wt[:, t, :], top[:, t, :], ACT.Exp, bias=ntop[:, t:t + 1],
                                     accum_out=wsum[:, t:t + 1]).then_inc(top_exped, 1)

            for n in range(3 * C):
                act.wait_ge(setup_full, n + 1)
                w, c = divmod(n, C)
                nc.scalar.activation((wqT, wkT, wvT)[w][0][:, c, :], psA[:, n % banks["A"], :], ACT.Copy,
                                     scale=float(D) ** -0.5 if w == 0 else 1.0).then_inc(setup_hi, 1)
            act.wait_ge(small_loaded, 16 * SMALL)
            act.wait_ge(setup_drained, FILLED)
            act.wait_ge(const_ready, 2)
            pipeline(act, {("A", "turn"): turn_hi, ("A", "mix"): mixed,
                           ("A", "qk"): qk, ("A", "value"): value, ("A", "score"): exp_scores, ("A", "prob"): probs_turned,
                           ("X", "ctx"): ctx_turned, ("X", "turn"): turn("X", "turn", xnxT), ("X", "query"): query,
                           ("X", "score"): x_exp, ("X", "prob"): x_probs_turned, ("X", "mix"): x_mixed,
                           ("F", "turn"): turn("F", "turn", xnfT), ("F", "route"): route, ("F", "score"): f_score,
                           ("F", "top"): f_top})

            act.wait_ge(steps["F"], F_STEPS * B)
            nc.scalar.activation(var_all[:, :], var_all[:, :], ACT.Ln, bias=1.0, accum_out=lsum[:, :])\
                .then_inc(log_done, 1)
            wait_drained(act, "F", FILL["F", "learn", 0], B - 1)
            nc.scalar.activation(gate[:, :], gate[:, :], ACT.Sigmoid, bias=b2c[:, 0:1]).then_inc(logit_done, 1)
            act.wait_ge(tail_step, 4)
            nc.scalar.activation(gate[:, :], gate[:, :], ACT.Sigmoid, scale=gwc[:, 0:1], bias=gbc[:, 0:1])\
                .then_inc(gate_ready, 1)
            with act.Fori(0, B // RING) as q:
                for k, (base_t, _) in enumerate(ring):
                    act.wait_ge(tail_added[k], q + 1)
                    act.dma_start(tiles(row(out, RING * q + k)), base_t[:, :, :]).then_inc(tail_stored[k], 16)
            for k in range(RING):
                act.wait_ge(tail_stored[k], 16 * (B // RING))

        @block.vector
        def _(dve):
            count = {}

            def mark(s, ins):
                ins.then_inc(steps[s], 1)
                count[s] += 1

            def settle(s, b):
                dve.wait_ge(steps[s], per_batch[s] * b + count[s])

            per_batch = {"A": A_STEPS, "X": X_STEPS, "F": F_STEPS, "G": G_STEPS}

            def norm(s, b, src, dst, normed):
                count[s] = 0
                for t in range(T):
                    last = nc.vector.bn_stats(stats[s][:, t, :], src[:, t, :])
                mark(s, last)
                settle(s, b)
                apart(dve)
                for t in range(T):
                    last = nc.vector.bn_aggr(mv[s][:, t, :], stats[s][:, t, :])
                mark(s, last)
                settle(s, b)
                mark(s, nc.vector.tensor_scalar(ve[s][:, :], mv[s][:, :, 1], EPS, None, ALU.add))
                settle(s, b)
                mark(s, nc.vector.tensor_scalar(rstd[s][:, :].bitcast(I32), ve[s][:, :].bitcast(I32), -0.5, RSQRT_SEED,
                                                ALU.mult, ALU.add))
                for _ in range(3):
                    settle(s, b)
                    mark(s, nc.vector.scalar_tensor_tensor(tmp[s][:, :], rstd[s][:, :], -0.5, ve[s][:, :], ALU.mult, ALU.mult))
                    settle(s, b)
                    mark(s, nc.vector.tensor_tensor(tmp[s][:, :], tmp[s][:, :], rstd[s][:, :], ALU.mult))
                    settle(s, b)
                    mark(s, nc.vector.scalar_tensor_tensor(rstd[s][:, :], tmp[s][:, :], 1.5, rstd[s][:, :], ALU.add, ALU.mult))
                settle(s, b)
                for t in range(T):
                    last = nc.vector.tensor_scalar(dst[:, t, :], src[:, t, :], mv[s][:, t, 0:1], rstd[s][:, t:t + 1],
                                                   ALU.subtract, ALU.mult)
                last.then_inc(normed, 1)

            def a_norm(b, _):
                if isinstance(b, int) and b == 0 and count:
                    return
                dve.wait_ge(x_loaded, 16 * (b + 1))
                norm("A", b, xa, xa, xa_normed)

            def x_norm(b, _):
                for t in range(T):
                    wait_drained(dve, "X", FILL["X", "enter", 0] + t, b)
                wait_full(dve, "X", FILL["X", "prob", 1] + 1, b - 1)
                norm("X", b, x1, xnx, x1_normed)

            def f_norm(b, _):
                for t in range(T):
                    wait_drained(dve, "X", FILL["X", "out", t], b)
                if isinstance(b, int) and b == B - 1:
                    wait_full(dve, "X", FILL["X", "prob", 1] + 1, b)
                else:
                    wait_full(dve, "X", FILL["X", "turn", 0] + 1, b + 1)
                wait(dve, base_ready, b)
                norm("F", b, x2, xnf, x2_normed)
                dve.wait_ge(x2_normed, b + 1)
                for t in range(T):
                    last = nc.vector.bn_stats(stats["F"][:, t, :], xnf[:, t, :])
                mark("F", last)
                settle("F", b)
                apart(dve)
                for t in range(T):
                    last = nc.vector.bn_aggr(mv["F"][:, t, :], stats["F"][:, t, :])
                mark("F", last)
                settle("F", b)
                mark("F", nc.vector.tensor_copy(columns(var_all, b), mv["F"][:, :, 1]))

            def lo(dst, src, hi):
                return nc.vector.tensor_tensor(dst, src, hi.bitcast(F32), ALU.subtract)

            def turn_lo(b, _):
                for j in range(2):
                    job = FILL["A", "turn", 0] + j
                    dve.wait_ge(xT_hi, 2 * b + j + 1)
                    part = slice(2 * j, 2 * j + 2)
                    lo(xT[1][:, part, :], bank("A", job)[:, 0:2 * S].rearrange("p (c s) -> p c s", c=2), xT[0][:, part, :])\
                        .then_inc(drained["A"][job % banks["A"]], 1)

            def qk(b, k):
                j = FILL["A", "qk", k]
                dve.wait_ge(qk_hi, NB * b + k + 1)
                for h in range(HB):
                    own = slice(h * DH, (h + 1) * DH)
                    lo(qm[1][own, k % 2, h, :], bank("A", j)[own, 0:S], qm[0][own, k % 2, h, :])
                lo(kT[1][:, k % 2, :], bank("A", j)[:, S:2 * S], kT[0][:, k % 2, :]).then_inc(drained["A"][j % banks["A"]], 1)

            def router_keys(b, _):
                if isinstance(b, int) and b == 0:
                    dve.wait_ge(mask_loaded, 16)
                    nc.vector.tensor_copy(rkS[:, :], rk32).then_inc(setup_drained, 1)
                    dve.wait_ge(setup_drained, FILLED + 1)
                    lo(rkL[:, :], rk32[0:RD + 1, :], rkS[0:RD + 1, :]).then_inc(setup_drained, 1)

            def maxima(b, u):
                for j in range(2):
                    job = FILL["A", "score", u] + j
                    wait_full(dve, "A", job, b)
                    nc.vector.tensor_reduce(nmax[:, u % 2, 2 * j:2 * j + 2],
                                            bank("A", job)[0:R, 0:2 * S].rearrange("p (h s) -> p h s", h=2),
                                            AX_X, ALU.max, negate=True).then_inc(a_maxed, 1)

            def share(b, u):
                for j in range(2):
                    wait_drained(dve, "A", FILL["A", "score", u] + j, b)
                mark("A", nc.vector.reciprocal(rsum[:, u, :], rsum[:, u, :]))
                settle("A", b)
                nc.vector.tensor_tensor(pa[:, :, :], pa[:, :, :], rsum[:, u, :].unsqueeze(2).to_broadcast([R, HB, S]),
                                        ALU.mult).then_inc(a_shared, 1)
                assert u < UNITS - 1 or count["A"] == A_STEPS

            def x_enter(b, _):
                dve.wait_ge(xr_biased, b + 1)
                for t in range(T):
                    wait_drained(dve, "X", FILL["X", "out", t], b - 1)
                for t in range(T):
                    j = FILL["X", "enter", 0] + t
                    wait_full(dve, "X", j, b)
                    nc.vector.tensor_tensor(x1[:, t, :], bank("X", j)[0:R, :], xr[:, t, :], ALU.add)\
                        .then_inc(drained["X"][j % banks["X"]], 1)

            def x_maxima(b, t):
                for j in range(2):
                    wait_full(dve, "X", FILL["X", "score", t] + j, b)
                nc.vector.tensor_reduce(xmax[:, t:t + 1], psX[0:R, :, 0:HK], AX_XY, ALU.max, negate=True).then_inc(x_maxed, 1)

            def x_probs_turned(b, t):
                j = FILL["X", "prob", t] + 1
                wait_full(dve, "X", j, b)
                nc.vector.tensor_copy(pxT[:, 3:6, t * R:(t + 1) * R], bank("X", j)[0:KP, 0:3 * R].rearrange("p (j q) -> p j q", j=3))\
                    .then_inc(drained["X"][j % banks["X"]], 1)

            def x_out(b, t):
                if t == 0:
                    mark("X", nc.vector.tensor_tensor(xrec[:, :], xsum[:, :, 0], xsum[:, :, 1], ALU.add))
                    settle("X", b)
                    mark("X", nc.vector.reciprocal(xrec[:, :], xrec[:, :]))
                    settle("X", b)
                    assert count["X"] == X_STEPS
                    dve.wait_ge(x1_biased, b + 1)
                    wait(dve, base_stored, 16 * b)
                j = FILL["X", "out", t]
                wait_full(dve, "X", j, b)
                nc.vector.scalar_tensor_tensor(x2[:, t, :], bank("X", j)[0:R, :], xrec[:, t:t + 1], x1[:, t, :],
                                               ALU.mult, ALU.add).then_inc(drained["X"][j % banks["X"]], 1)

            def route(b, _):
                j = FILL["F", "route", 0]
                dve.wait_ge(rq_hi, b + 1)
                lo(rqS[LO:RS, :], bank("F", j)[LO:RS, 0:S], rqS[LO:RS, :]).then_inc(drained["F"][j % banks["F"]], 1)

            def learn(b, _):
                j = FILL["F", "learn", 0]
                wait_full(dve, "F", j, b)
                nc.vector.tensor_copy(columns(gate, b), bank("F", j)[0:R, 0:T]).then_inc(drained["F"][j % banks["F"]], 1)

            def f_top(b, t):
                for n in range(2):
                    wait_drained(dve, "F", FILL["F", "score", 2 * t + 1] + n, b)
                apart(dve)
                mark("F", nc.vector.max(top[:, t, :], sc[0:R, :]))
                settle("F", b)
                nc.vector.tensor_scalar(ntop[:, t:t + 1], top[:, t, 0:1], -1.0, None, ALU.mult).then_inc(top_ready, 1)
                nc.vector.max_index(idx[:, t, :], top[:, t, :], sc[0:R, :]).then_inc(sc_searched, 1)
                assert t == 0 or count["F"] == F_STEPS

            def g_sum(b, c):
                t, part = divmod(c, PARTS)
                if c == 0:
                    count["G"] = 0
                if part == 0:
                    dve.wait_ge(top_exped, T * b + t + 1)
                    mark("G", nc.vector.reciprocal(wsum[:, t:t + 1], wsum[:, t:t + 1]))
                    settle("G", b)
                    mark("G", nc.vector.tensor_scalar(wt[:, t, :], wt[:, t, :], wsum[:, t:t + 1], None, ALU.mult))
                    settle("G", b)
                    wait(dve, agg_stored, 16 * (T * b + t))
                else:
                    dve.wait_ge(summed, CHUNKS * b + c)
                dve.wait_ge(gathered, 16 * KG * (CHUNKS * b + c + 1))
                for k in range(KG):
                    w = wt[:, t, KG * part + k:KG * part + k + 1]
                    if part == 0 and k == 0:
                        last = nc.vector.tensor_scalar(agg[:, :], vgv[:, k, :], w, None, ALU.mult)
                    else:
                        last = nc.vector.scalar_tensor_tensor(agg[:, :], vgv[:, k, :], w, agg[:, :], ALU.mult, ALU.add)
                    if k < KG - 1:
                        mark("G", last)
                        settle("G", b)
                last.then_inc(summed, 1)
                assert c < CHUNKS - 1 or count["G"] == G_STEPS

            fills = [0]

            def made():
                dve.wait_ge(setup_full, fills[0] + 1)
                fills[0] += 1
                return psA[:, (fills[0] - 1) % banks["A"], :]

            for w, scale in ((wqT, float(D) ** -0.5), (wkT, 1.0), (wvT, 1.0)):
                for c in range(C):
                    dve.wait_ge(setup_hi, fills[0] + 1)
                    nc.vector.scalar_tensor_tensor(w[1][:, c, :], made(), scale, w[0][:, c, :].bitcast(F32),
                                                   ALU.mult, ALU.subtract).then_inc(setup_drained, 1)
            for c in range(C):
                nc.vector.tensor_copy(wffT[:, c, :], made()).then_inc(setup_drained, 1)
            for c in range(C):
                nc.vector.tensor_copy(woT[:, c, :], made()).then_inc(setup_drained, 1)
            dve.wait_ge(small_loaded, 16 * SMALL)
            nc.vector.tensor_copy(bv_rows, bvc[:, :].unsqueeze(2).to_broadcast([P, C, R])).then_inc(small_step, 1)
            a_norm(0, 0)
            for c in range(C):
                nc.vector.tensor_copy(m2v[:, c, :], made()).then_inc(setup_drained, 1)
            nc.vector.tensor_tensor(cb[:, :], made()[0:R, :], cb[:, :], ALU.add).then_inc(setup_drained, 1)
            for c in range(C):
                nc.vector.tensor_scalar(m1v[:, c, :], made(), float(D) ** -0.5, None, ALU.mult).then_inc(setup_drained, 1)
            nc.vector.tensor_scalar(gb[:, :], made()[:, 0:C], float(D) ** -0.5, None, ALU.mult).then_inc(setup_drained, 1)
            dve.wait_ge(const_ready, 2)
            src = made()
            nc.vector.tensor_copy(rwT[:, 0:RD], src[:, 0:RD])
            nc.vector.tensor_copy(rwT[:, LO:RS], src[:, 0:RD]).then_inc(setup_drained, 1)
            src = made()[:, 0:C * RD].rearrange("p (c r) -> p c r", c=C)
            nc.vector.tensor_copy(routeT[:, :, 0:RD], src)
            nc.vector.tensor_copy(routeT[:, :, LO:RS], src).then_inc(setup_drained, 1)
            for n in range(4):
                nc.vector.tensor_copy(keysT[:, n * BANK:(n + 1) * BANK], made()).then_inc(setup_drained, 1)
            for n in range(4):
                nc.vector.tensor_scalar(rk32[:, n * BANK:(n + 1) * BANK], made()[0:RS, :], float(RD) ** -0.5, None,
                                        ALU.mult).then_inc(setup_drained, 1)
            nc.vector.tensor_copy(unc1T[:, :, :], made().rearrange("p (c f) -> p c f", c=C)).then_inc(setup_drained, 1)
            assert fills[0] == FILLED
            pipeline(dve, {("A", "norm"): a_norm, ("A", "value"): router_keys, ("A", "turn"): turn_lo, ("A", "qk"): qk,
                           ("A", "score"): maxima, ("A", "share"): share,
                           ("X", "enter"): x_enter,
                           ("X", "norm"): x_norm, ("X", "score"): x_maxima, ("X", "prob"): x_probs_turned, ("X", "out"): x_out,
                           ("F", "norm"): f_norm, ("F", "route"): route, ("F", "learn"): learn, ("F", "top"): f_top,
                           ("G", "sum"): g_sum})

            dve.wait_ge(log_done, 1)
            nc.vector.tensor_copy(lsums, lsum[:, :].to_broadcast([R, R])).then_inc(lsum_spread, 1)
            dve.wait_ge(mean_full, 1)
            nc.vector.tensor_scalar(rmean[:, :], bank("F", 0)[0:R, 0:1], 1.0 / (B * S), 1e-6, ALU.mult, ALU.add).then_inc(tail_step, 1)
            dve.wait_ge(tail_step, 1)
            nc.vector.reciprocal(rmean[:, :], rmean[:, :]).then_inc(tail_step, 1)
            dve.wait_ge(tail_step, 2)
            nc.vector.tensor_scalar(var_all[:, :], var_all[:, :], rmean[:, 0:1], 0.5, ALU.mult, ALU.mult).then_inc(tail_step, 1)
            dve.wait_ge(tail_step, 3)
            dve.wait_ge(logit_done, 1)
            nc.vector.scalar_tensor_tensor(gate[:, :], gate[:, :], 2.5, var_all[:, :], ALU.mult, ALU.add).then_inc(clip_ready, 1)
            dve.wait_ge(clip_ready, 1)
            nc.vector.tensor_scalar(gate[:, :], gate[:, :], 0.0, 5.0, ALU.max, ALU.min).then_inc(tail_step, 1)
            dve.wait_ge(gate_ready, 1)

            for n in range(B):
                base_t, agg_t = ring[n % RING]
                dve.wait_ge(tail_loaded[n % RING], 32 * (n // RING) + 32)
                for t in range(T):
                    last = nc.vector.scalar_tensor_tensor(base_t[:, t, :], agg_t[:, t, :], gate[:, T * n + t:T * n + t + 1],
                                                          base_t[:, t, :], ALU.mult, ALU.add)
                last.then_inc(tail_added[n % RING], 1)
                if n % 3 == 2 and n // 3 < CHUNKS:
                    g_sum(B - 1, n // 3)

        @block.tensor
        def _(pe):
            def product(dst, pairs):
                for n, (stationary, moving) in enumerate(pairs):
                    last = nc.tensor.matmul(dst, stationary, moving, start=n == 0, stop=n == len(pairs) - 1)
                return last

            def product3(dst, pairs):
                return product(dst, [p for s, m in pairs for p in ((s[0], m[0]), (s[0], m[1]), (s[1], m[0]))])

            def turned(dst, src):
                k = src.shape[0]
                return nc.tensor.transpose(dst, src, ident[0:k, 0:k])

            def filled(s, j, last):
                last.then_inc(full[s][j % banks[s]], 1)

            def both(parts, *at):
                return tuple(part[at] for part in parts)

            def turn(s, name, src, ready):
                def step(b, _):
                    ready(b)
                    for j in range(2):
                        job = FILL[s, name, 0] + j
                        wait_free(pe, s, job, b)
                        for k in range(2):
                            for t in range(T):
                                at, c = k * S + t * R, 2 * j + k
                                last = turned(bank(s, job)[:, at:at + R], src[:, t, c * P:(c + 1) * P])
                        filled(s, job, last)
                return step

            def normed(what):
                return lambda b: pe.wait_ge(what, b + 1)

            def qk(b, k):
                if k == 0:
                    wait_drained(pe, "A", FILL["A", "turn", 0] + 1, b)
                j = FILL["A", "qk", k]
                wait_free(pe, "A", j, b)
                for n, w in enumerate((wqT, wkT)):
                    last = product3(bank("A", j)[:, n * S:(n + 1) * S],
                                    [(both(w, ALL, c, slice(k * P, (k + 1) * P)), both(xT, ALL, c, ALL)) for c in range(C)])
                filled("A", j, last)

            def value(b, _):
                wait_drained(pe, "A", FILL["A", "turn", 0] + 1, b)
                for t in range(T):
                    j = FILL["A", "value", 0] + t
                    wait_free(pe, "A", j, b)
                    filled("A", j, product3(bank("A", j)[0:R, :], [(both(xT, ALL, c, slice(t * R, (t + 1) * R)),
                                                                    both(wvT, ALL, c, ALL)) for c in range(C)]))

            def scores(b, u):
                k, t = divmod(u, T)
                wait_drained(pe, "A", FILL["A", "qk", k], b)
                for j in range(2):
                    job = FILL["A", "score", u] + j
                    wait_free(pe, "A", job, b)
                    for h in range(2):
                        last = product3(bank("A", job)[0:R, h * S:(h + 1) * S],
                                        [(both(qm, ALL, k % 2, 2 * j + h, slice(t * R, (t + 1) * R)), both(kT, ALL, k % 2, ALL))])
                    filled("A", job, last)

            def probs(b, u):
                pe.wait_ge(a_shared, UNITS * b + u + 1)
                for t in range(T):
                    j = FILL["A", "prob", u] + t
                    wait_free(pe, "A", j, b)
                    for h in range(HB):
                        last = turned(bank("A", j)[0:R, h * R:(h + 1) * R], pa[:, h, t * R:(t + 1) * R])
                    filled("A", j, last)

            def mixed(b, u):
                k, j = u // T, FILL["A", "mix", u]
                wait_drained(pe, "A", FILL["A", "prob", u] + 1, b)
                wait_free(pe, "A", j, b)
                for t in range(T):
                    for h in range(HB):
                        last = nc.tensor.matmul(bank("A", j)[h * DH:(h + 1) * DH, 0:R], va[:, t, HB * k + h, :],
                                                paT[:, u % 2, t, h, :], start=t == 0, stop=t == T - 1)
                filled("A", j, last)

            def enter(b, _):
                wait_drained(pe, "A", FILL["A", "mix", UNITS - 1], b)
                for t in range(T):
                    j = FILL["X", "enter", 0] + t
                    wait_free(pe, "X", j, b)
                    filled("X", j, product(bank("X", j)[0:R, :],
                                           [(oT[:, c, t * R:(t + 1) * R], wffT[:, c, :]) for c in range(C)]))

            def ctx_turn(b, c):
                if c == 0:
                    pe.wait_ge(ctx_loaded, 16 * (b + 1))
                for half in range(2):
                    j = FILL["X", "ctx", c] + half
                    wait_free(pe, "X", j, b)
                    for k in range(3):
                        last = turned(bank("X", j)[:, k * KP:(k + 1) * KP], cxv[:, 3 * half + k, c * P:(c + 1) * P])
                    filled("X", j, last)

            def query(b, _):
                wait_drained(pe, "X", FILL["X", "turn", 0] + 1, b)
                for j in range(2):
                    job = FILL["X", "query", 0] + j
                    wait_free(pe, "X", job, b)
                    for k in range(2):
                        i = 2 * j + k
                        last = product(bank("X", job)[:, k * S:(k + 1) * S],
                                       [(m1v[:, c, i * P:(i + 1) * P], xnxT[:, c, :]) for c in range(C)])
                    filled("X", job, last)

            def x_scores(b, t):
                if t == 0:
                    for j in range(2):
                        wait_drained(pe, "X", FILL["X", "query", 0] + j, b)
                for j in range(2):
                    job = FILL["X", "score", t] + j
                    wait_free(pe, "X", job, b)
                    filled("X", job, product(bank("X", job)[0:R, 0:HK],
                                             [(gT[:, c, t * R:(t + 1) * R], cxT[:, c, j * HK:(j + 1) * HK]) for c in range(C)]))

            def x_probs(b, t):
                for j in range(2):
                    wait_drained(pe, "X", FILL["X", "score", t] + j, b)
                for j in range(2):
                    job = FILL["X", "prob", t] + j
                    wait_free(pe, "X", job, b)
                    for k in range(3):
                        n = 3 * j + k
                        last = turned(bank("X", job)[0:KP, k * R:(k + 1) * R], px[:, t, n * KP:(n + 1) * KP])
                    filled("X", job, last)

            def x_mix(b, part):
                if part == 0:
                    for j in range(2):
                        wait_drained(pe, "X", FILL["X", "prob", 1] + j, b)
                job = FILL["X", "mix", part]
                wait_free(pe, "X", job, b)
                for k in range(2):
                    i = 2 * part + k
                    last = product(bank("X", job)[:, k * S:(k + 1) * S],
                                   [(cxv[:, n, i * P:(i + 1) * P], pxT[:, n, :]) for n in range(KC)])
                filled("X", job, last)

            def x_out(b, t):
                if t == 0:
                    wait_drained(pe, "X", FILL["X", "mix", 1], b)
                job = FILL["X", "out", t]
                wait_free(pe, "X", job, b)
                filled("X", job, product(bank("X", job)[0:R, :],
                                         [(uT[:, c, t * R:(t + 1) * R], m2v[:, c, :]) for c in range(C)]))

            def route(b, _):
                wait_drained(pe, "F", FILL["F", "turn", 0] + 1, b)
                j = FILL["F", "route", 0]
                wait_free(pe, "F", j, b)
                product(bank("F", j)[0:RS, 0:S], [(routeT[:, c, :], xnfT[:, c, :]) for c in range(C)])
                filled("F", j, product(bank("F", j)[:, S:2 * S], [(unc1T[:, c, :], xnfT[:, c, :]) for c in range(C)]))

            def learn(b, _):
                wait_drained(pe, "F", FILL["F", "route", 0], b)
                j = FILL["F", "learn", 0]
                wait_free(pe, "F", j, b)
                for t in range(T):
                    last = product(bank("F", j)[0:R, t:t + 1], [(h1[:, t * R:(t + 1) * R], w2c[:, :])])
                filled("F", j, last)

            def f_scores(b, part):
                t, half = divmod(part, 2)
                tile = slice(t * R, (t + 1) * R)
                for n in (2 * half, 2 * half + 1):
                    j = FILL["F", "score", part] + n % 2
                    cols = slice(n * BANK, (n + 1) * BANK)
                    wait_free(pe, "F", j, b)
                    filled("F", j, product(bank("F", j)[0:R, :],
                                           [(rqS[:, tile], rkS[:, cols]), (rqS[0:RD + 1, tile], rkL[:, cols])]))

            fills = [0]

            def place():
                wait(pe, setup_drained, fills[0] - banks["A"] + 1)
                fills[0] += 1
                return psA[:, (fills[0] - 1) % banks["A"], :]

            def turn_weight(w):
                for i in range(C):
                    dst = place()
                    for o in range(C):
                        last = turned(dst[:, o * P:(o + 1) * P], w[:, o, i * P:(i + 1) * P])
                    last.then_inc(setup_full, 1)

            pe.wait_ge(const_ready, 1)
            for n, w in enumerate((at_cx, at_m1, at_sc, at_big, at_m2)):
                pe.wait_ge(weight_loaded[n], 16)
                turn_weight(w)
            pe.wait_ge(cross_loaded[1], 16)
            pe.wait_ge(setup_drained, WO)
            for i in range(C):
                product(place(), [(at_m1[:, e, i * P:(i + 1) * P], woT[:, e, :]) for e in range(C)]).then_inc(setup_full, 1)
            pe.wait_ge(small_step, 1)
            product(place()[0:R, :], [(bv_rows[:, e, :], woT[:, e, :]) for e in range(C)]).then_inc(setup_full, 1)
            pe.wait_ge(cross_loaded[0], 16)
            pe.wait_ge(cross_loaded[2], 16)
            for i in range(C):
                product(place(), [(at_sc[:, e, i * P:(i + 1) * P], at_cx[:, e, :]) for e in range(C)]).then_inc(setup_full, 1)
            dst = place()
            for i in range(C):
                last = product(dst[:, i:i + 1], [(at_cx[:, e, i * P:(i + 1) * P], bqc[:, e:e + 1]) for e in range(C)])
            last.then_inc(setup_full, 1)
            pe.wait_ge(look_up_loaded, 16 * 4)
            turned(place()[:, 0:RD], rw).then_inc(setup_full, 1)
            pe.wait_ge(setup_drained, fills[0])
            dst = place()
            for i in range(C):
                last = product(dst[:, i * RD:(i + 1) * RD], [(qw[:, i * P:(i + 1) * P], rwT[:, 0:RD])])
            last.then_inc(setup_full, 1)
            for n in range(4):
                dst = place()
                for k in range(4):
                    last = turned(dst[:, k * P:(k + 1) * P], keys[:, 4 * n + k, :])
                last.then_inc(setup_full, 1)
            pe.wait_ge(setup_drained, fills[0])
            for n in range(4):
                product(place()[0:RS, :], [(rwT, keysT[:, n * BANK:(n + 1) * BANK])]).then_inc(setup_full, 1)
            dst = place()
            for i in range(C):
                last = turned(dst[:, i * P:(i + 1) * P], uw1[:, i * P:(i + 1) * P])
            last.then_inc(setup_full, 1)
            pe.wait_ge(setup_drained, FILLED)

            pipeline(pe, {("A", "turn"): turn("A", "turn", xa, normed(xa_normed)),
                          ("X", "turn"): turn("X", "turn", xnx, normed(x1_normed)),
                          ("F", "turn"): turn("F", "turn", xnf, normed(x2_normed)),
                          ("A", "qk"): qk, ("A", "value"): value, ("A", "score"): scores,
                          ("A", "prob"): probs, ("A", "mix"): mixed, ("X", "enter"): enter,
                          ("X", "ctx"): ctx_turn, ("X", "query"): query, ("X", "score"): x_scores,
                          ("X", "prob"): x_probs, ("X", "mix"): x_mix, ("X", "out"): x_out,
                          ("F", "route"): route, ("F", "learn"): learn, ("F", "score"): f_scores})

            pe.wait_ge(lsum_spread, 1)
            wait_free(pe, "F", 0, B)
            product(bank("F", 0)[0:R, 0:1], [(lsums, one[:, :])]).then_inc(mean_full, 1)


_INS = ['x', 'ctx_1024', 'L0_attn_Wq', 'L0_attn_Wk', 'L0_attn_Wv', 'L0_attn_Wff', 'L0_attn_bff', 'L0_xattn_Wk',
        'L0_xattn_Wv', 'L0_xattn_bv', 'L0_xattn_Wq', 'L0_xattn_bq', 'L0_xattn_Wo', 'L0_xattn_bo',
        'L0_ffn_q_proj_w', 'L0_ffn_router_w', 'L0_ffn_aux_keys', 'L0_ffn_aux_values', 'L0_ffn_reliability_mask',
        'L0_ffn_unc_w1', 'L0_ffn_unc_b1', 'L0_ffn_unc_w2', 'L0_ffn_unc_b2', 'L0_ffn_gate_w1', 'L0_ffn_gate_bias']


def kernel(**inputs):
    import numpy as np
    import concourse.bacc as bacc
    from concourse.bass_utils import run_bass_kernel_spmd

    nc = bacc.Bacc("TRN2", target_bir_lowering=False, num_devices=1)
    arrays, args = {}, []
    for name in _INS:
        a = np.ascontiguousarray(inputs[name])
        if a.ndim == 0:
            a = a.reshape(1)
        arrays[f"in_{name}"] = a
        args.append(nc.dram_tensor(f"in_{name}", a.shape, mybir.dt.from_np(a.dtype), kind="ExternalInput").ap())
    out = nc.dram_tensor("out", [B, S, D], F32, kind="ExternalOutput").ap()
    build(nc, *args, out)
    return run_bass_kernel_spmd(nc, [arrays], core_ids=[0]).results[0]["out"]
```
